# Optimizing a Trainium2 kernel written in Bass

```python
import numpy as np
import jax
import jax.numpy as jnp

def _softmax(x, axis=-1):
    return jax.nn.softmax(x, axis=axis)

def _gelu(x):
    return jax.nn.gelu(x, approximate=True)

def _silu(x):
    return jax.nn.silu(x)

def _sigmoid(x):
    return jax.nn.sigmoid(x)

def _layernorm(x, axis=-1, eps=1e-05):
    m = jnp.mean(x, axis=axis, keepdims=True)
    v = jnp.var(x, axis=axis, keepdims=True)
    return (x - m) / jnp.sqrt(v + eps)

def _scatter_add(tgt, idx, src, axis=0):
    return tgt.at[idx].add(src)

def _segment_sum(src, seg, n):
    return jax.ops.segment_sum(src, seg, n)
kernel_name = 'mk_adj_resnorm_d4_adj_r2_d897fa'

def setup_inputs(seed: int=0):
    np.random.seed(seed)
    _w = jnp.asarray

    def _rec_inputs():
        import jax
        import jax.numpy as jnp
        _gk = jax.random.key(seed)
        x = -0.0003929 + 0.9999 * jax.random.normal(jax.random.fold_in(_gk, 1), (8, 1024, 128), jnp.float32)
        _w = (1.0 + jnp.arange(1024, dtype=jnp.float32)) ** (-0.5)
        _w = _w / _w.mean()
        _pij = jnp.clip(0.00195312 * _w[:, None] * _w[None, :], 0.0, 1.0)
        _a = jax.random.uniform(jax.random.fold_in(_gk, 2), (1024, 1024)) < _pij
        _a = jnp.logical_or(_a, jnp.eye(1024, dtype=bool))
        _af = _a.astype(jnp.float32)
        _af = _af * jax.random.uniform(jax.random.fold_in(_gk, 3), (1024, 1024), jnp.float32, 0.05, 0.00012207)
        adj = _af
        return (x, adj)
    x, adj = _rec_inputs()

    def _L0_gnn_setup():
        import jax, jax.numpy as jnp
        import numpy as np
        key = jax.random.key(seed)
        k1, k2, k3, k4 = jax.random.split(key, 4)
        B, N, F_in, F_out = (16, 4096, 128, 128)
        x = jax.random.normal(k1, (B, N, F_in), dtype=jnp.float32)
        adj = jax.random.uniform(k2, (N, N), dtype=jnp.float32) / N
        stdv = 1.0 / np.sqrt(F_in)
        weight = jax.random.uniform(k3, (F_in, F_out), dtype=jnp.float32, minval=-stdv, maxval=stdv)
        bias = jax.random.uniform(k4, (F_out,), dtype=jnp.float32, minval=-stdv, maxval=stdv)
        return {'x': x, 'adj': adj, 'weight': weight, 'bias': bias}
    _L0_gnn_all = _L0_gnn_setup()
    _L0_gnn_in = {k: v for k, v in _L0_gnn_all.items() if k in ('weight', 'bias')}
    del _L0_gnn_all

    def _L1_gnn_setup():
        import jax, jax.numpy as jnp
        import numpy as np
        B, N, D, OUT = (8, 1024, 128, 128)
        key = jax.random.key(seed)
        k1, k2, k3, k4, k5, k6 = jax.random.split(key, 6)
        stdv = 1.0 / np.sqrt(OUT)
        inputs = jax.random.normal(k1, (B, N, D), dtype=jnp.float32)
        relation = jax.random.normal(k2, (N, N), dtype=jnp.float32)
        gl = 1.0 / np.sqrt(2 * D + 1)
        g_w = jax.random.uniform(k3, (2 * D + 1,), minval=-gl, maxval=gl, dtype=jnp.float32)
        g_b = jax.random.uniform(k4, (), minval=-gl, maxval=gl, dtype=jnp.float32)
        weight = jax.random.uniform(k5, (D, OUT), minval=-stdv, maxval=stdv, dtype=jnp.float32)
        bias = jax.random.uniform(k6, (OUT,), minval=-stdv, maxval=stdv, dtype=jnp.float32)
        return {'inputs': inputs, 'relation': relation, 'g_w': g_w, 'g_b': g_b, 'weight': weight, 'bias': bias}
    _L1_gnn_all = _L1_gnn_setup()
    _L1_gnn_in = {k: v for k, v in _L1_gnn_all.items() if k in ('g_w', 'g_b', 'weight', 'bias')}
    del _L1_gnn_all

    def _L2_gnn_setup():
        import jax, jax.numpy as jnp
        import numpy as np
        ALPHA = 0.005

        def _linear_init(key, fan_in, shape):
            bound = 1.0 / np.sqrt(fan_in)
            return jax.random.uniform(key, shape, jnp.float32, -bound, bound)
        key = jax.random.key(seed)
        ks = jax.random.split(key, 12)
        B, N, NI, NH, NO = (4, 256, 128, 128, 128)
        x = jax.random.normal(ks[0], (B, N, NI), jnp.float32)
        adj = (jax.random.uniform(ks[1], (N, N)) < 0.05).astype(jnp.float32)
        Wi = _linear_init(ks[2], NI, (NI, NH))
        bi = _linear_init(ks[3], NI, (NH,))
        We = _linear_init(ks[4], 2 * NH, (2 * NH, 1))
        be = _linear_init(ks[5], 2 * NH, (1,))
        Wn = _linear_init(ks[6], 2 * NH, (2 * NH, NO))
        bn = _linear_init(ks[7], 2 * NH, (NO,))
        Wm = _linear_init(ks[8], 2 * NH, (2 * NH, NO))
        bm = _linear_init(ks[9], 2 * NH, (NO,))
        return {'x': x, 'adj': adj, 'Wi': Wi, 'bi': bi, 'We': We, 'be': be, 'Wn': Wn, 'bn': bn, 'Wm': Wm, 'bm': bm}
    _L2_gnn_all = _L2_gnn_setup()
    _L2_gnn_in = {k: v for k, v in _L2_gnn_all.items() if k in ('Wi', 'bi', 'We', 'be', 'Wn', 'bn', 'Wm', 'bm')}
    del _L2_gnn_all

    def _L3_gnn_setup():
        import jax, jax.numpy as jnp
        import numpy as np
        B, N, D = (32, 512, 128)
        TIME_STEP = 5
        key = jax.random.key(seed)
        ks = jax.random.split(key, 12)
        s2 = 1.0 / np.sqrt(2 * D)
        s1 = 1.0 / np.sqrt(D)
        return {'input': jax.random.normal(ks[0], (B, N, D), jnp.float32), 'in_matrix': jax.random.uniform(ks[1], (N, N), jnp.float32), 'out_matrix': jax.random.uniform(ks[2], (N, N), jnp.float32), 'w3_w': jax.random.normal(ks[3], (D, 2 * D), jnp.float32) * s2, 'w3_b': jnp.zeros((D,), jnp.float32), 'u3_w': jax.random.normal(ks[4], (D, D), jnp.float32) * s1, 'u3_b': jnp.zeros((D,), jnp.float32), 'w4_w': jax.random.normal(ks[5], (D, 2 * D), jnp.float32) * s2, 'w4_b': jnp.zeros((D,), jnp.float32), 'w5_w': jax.random.normal(ks[6], (D, 2 * D), jnp.float32) * s2, 'w5_b': jnp.zeros((D,), jnp.float32), 'u5_w': jax.random.normal(ks[7], (D, D), jnp.float32) * s1, 'u5_b': jnp.zeros((D,), jnp.float32), 'time_step': TIME_STEP}
    _L3_gnn_all = _L3_gnn_setup()
    _L3_gnn_in = {k: v for k, v in _L3_gnn_all.items() if k in ('w3_w', 'w3_b', 'u3_w', 'u3_b', 'w4_w', 'w4_b', 'w5_w', 'w5_b', 'u5_w', 'u5_b')}
    del _L3_gnn_all
    return {'x': x, 'adj': adj, 'L0_gnn_weight': _L0_gnn_in['weight'], 'L0_gnn_bias': _L0_gnn_in['bias'], 'L1_gnn_g_w': _L1_gnn_in['g_w'], 'L1_gnn_g_b': _L1_gnn_in['g_b'], 'L1_gnn_weight': _L1_gnn_in['weight'], 'L1_gnn_bias': _L1_gnn_in['bias'], 'L2_gnn_Wi': _L2_gnn_in['Wi'], 'L2_gnn_bi': _L2_gnn_in['bi'], 'L2_gnn_We': _L2_gnn_in['We'], 'L2_gnn_be': _L2_gnn_in['be'], 'L2_gnn_Wn': _L2_gnn_in['Wn'], 'L2_gnn_bn': _L2_gnn_in['bn'], 'L2_gnn_Wm': _L2_gnn_in['Wm'], 'L2_gnn_bm': _L2_gnn_in['bm'], 'L3_gnn_w3_w': _L3_gnn_in['w3_w'], 'L3_gnn_w3_b': _L3_gnn_in['w3_b'], 'L3_gnn_u3_w': _L3_gnn_in['u3_w'], 'L3_gnn_u3_b': _L3_gnn_in['u3_b'], 'L3_gnn_w4_w': _L3_gnn_in['w4_w'], 'L3_gnn_w4_b': _L3_gnn_in['w4_b'], 'L3_gnn_w5_w': _L3_gnn_in['w5_w'], 'L3_gnn_w5_b': _L3_gnn_in['w5_b'], 'L3_gnn_u5_w': _L3_gnn_in['u5_w'], 'L3_gnn_u5_b': _L3_gnn_in['u5_b']}

def reference(x, adj, L0_gnn_weight, L0_gnn_bias, L1_gnn_g_w, L1_gnn_g_b, L1_gnn_weight, L1_gnn_bias, L2_gnn_Wi, L2_gnn_bi, L2_gnn_We, L2_gnn_be, L2_gnn_Wn, L2_gnn_bn, L2_gnn_Wm, L2_gnn_bm, L3_gnn_w3_w, L3_gnn_w3_b, L3_gnn_u3_w, L3_gnn_u3_b, L3_gnn_w4_w, L3_gnn_w4_b, L3_gnn_w5_w, L3_gnn_w5_b, L3_gnn_u5_w, L3_gnn_u5_b):
    import jax
    import jax.numpy as jnp

    def _L0_gnn_ref(x, adj, weight, bias):
        import jax, jax.numpy as jnp
        import numpy as np
        support = jnp.einsum('bnf,fo->bno', x, weight)
        output = jnp.einsum('nm,bmo->bno', adj, support)
        return output + bias

    def _L1_gnn_ref(inputs, relation, g_w, g_b, weight, bias):
        import jax, jax.numpy as jnp
        import numpy as np
        B, N, D, OUT = (8, 1024, 128, 128)
        b, n, d = inputs.shape
        w_j = g_w[:d]
        w_i = g_w[d:2 * d]
        w_r = g_w[2 * d]
        sj = inputs @ w_j
        si = inputs @ w_i
        res = si[:, :, None] + sj[:, None, :] + relation[None] * w_r + g_b
        agg = jnp.einsum('bij,bjd->bid', res, inputs)
        return agg @ weight + bias

    def _L2_gnn_ref(x, adj, Wi, bi, We, be, Wn, bn, Wm, bm):
        import jax, jax.numpy as jnp
        import numpy as np
        ALPHA = 0.005

        def _linear_init(key, fan_in, shape):
            bound = 1.0 / np.sqrt(fan_in)
            return jax.random.uniform(key, shape, jnp.float32, -bound, bound)
        H = Wi.shape[1]
        x_h = jax.nn.elu(x @ Wi + bi)
        a_src = x_h @ We[:H, 0]
        a_tgt = x_h @ We[H:, 0]
        e = jax.nn.sigmoid(a_tgt[:, :, None] + a_src[:, None, :] + be[0])
        mask = adj + ALPHA * (1.0 - (adj != 0).astype(adj.dtype))
        e = e * mask
        agg = jnp.einsum('bij,bjh->bih', e, x_h)
        self_part = x_h * jnp.sum(e, axis=-1, keepdims=True)
        recv = jnp.concatenate([agg, self_part], axis=-1)
        recv = jax.nn.elu(recv @ Wn + bn)
        out = jnp.concatenate([recv, x_h], axis=-1) @ Wm + bm
        return out

    def _L3_gnn_ref(input, in_matrix, out_matrix, w3_w, w3_b, u3_w, u3_b, w4_w, w4_b, w5_w, w5_b, u5_w, u5_b, time_step):
        import jax, jax.numpy as jnp
        import numpy as np
        B, N, D = (32, 512, 128)
        TIME_STEP = 5

        def step(h, _):
            m_in = jnp.einsum('nm,bmd->bnd', in_matrix, h)
            m_out = jnp.einsum('nm,bmd->bnd', out_matrix, h)
            av = jnp.concatenate([m_in, m_out], axis=-1)
            u3 = h @ u3_w.T + u3_b
            z = jax.nn.sigmoid(av @ w3_w.T + w3_b + u3)
            r = jax.nn.sigmoid(av @ w4_w.T + w4_b + u3)
            hv = jnp.tanh(av @ w5_w.T + w5_b + (r * h @ u5_w.T + u5_b))
            h = (1.0 - z) * h + z * hv
            return (h, None)
        h, _ = jax.lax.scan(step, input, None, length=time_step)
        return h
    x = _layernorm(x + _L0_gnn_ref(x, adj, L0_gnn_weight, L0_gnn_bias), axis=-1)
    x = _layernorm(x + _L1_gnn_ref(x, adj, L1_gnn_g_w, L1_gnn_g_b, L1_gnn_weight, L1_gnn_bias), axis=-1)
    x = _layernorm(x + _L2_gnn_ref(x, adj, L2_gnn_Wi, L2_gnn_bi, L2_gnn_We, L2_gnn_be, L2_gnn_Wn, L2_gnn_bn, L2_gnn_Wm, L2_gnn_bm), axis=-1)
    x = _layernorm(x + _L3_gnn_ref(x, adj, adj, L3_gnn_w3_w, L3_gnn_w3_b, L3_gnn_u3_w, L3_gnn_u3_b, L3_gnn_w4_w, L3_gnn_w4_b, L3_gnn_w5_w, L3_gnn_w5_b, L3_gnn_u5_w, L3_gnn_u5_b, 5), axis=-1)
    return x

_drawn_inputs = setup_inputs


def setup_inputs(seed=0):
    import zlib

    import numpy as np

    out = dict(_drawn_inputs(seed))
    spreads = {'L3_gnn_w3_b': (0.0, 0.543),
     'L3_gnn_u3_b': (0.0, 0.605),
     'L3_gnn_w4_b': (0.0, 0.8),
     'L3_gnn_w5_b': (0.0, 0.1),
     'L3_gnn_u5_b': (0.0, 0.1)}
    factors = {'L1_gnn_bias': 24.527, 'L2_gnn_bn': 4.478, 'L3_gnn_w3_w': 4.842, 'L3_gnn_w4_w': 8.0}
    for name, (base, spread) in spreads.items():
        noise = np.random.default_rng([zlib.crc32(name.encode()), seed]).standard_normal(out[name].shape)
        drawn = base * np.exp(spread * noise) if base else spread * noise
        out[name] = jnp.asarray(drawn.astype(out[name].dtype))
    for name, factor in factors.items():
        out[name] = (out[name] * factor).astype(out[name].dtype)
    return out
```

```python
from contextlib import ExitStack

import concourse.bass as bass
from concourse import mybir

P = 128
HALF = 512
ALPHA = 0.005
EPS = 1e-5
STEPS = 5

ALU = mybir.AluOpType
ACT = mybir.ActivationFunctionType
F32 = mybir.dt.float32
F32R = mybir.dt.float32r

(W0, W1R, WI, WNA, WNB, WMA, WMB, U3, W3, WD, W5, U5) = range(12)
RAW0 = ["W0", "W1", "Wi", "WnA", "WnB", "WmA", "WmB", "u3"]
RAW1 = ["w3a", "w3b", "w4a", "w4b", "w5a", "w5b", "u5"]
MB, GB, VB, TB = 0, 2, 4, 6


def program(nc, x_in, adjT, w, out):
    B, N, D = x_in.shape
    T = N // P
    PAIRS = B // 2
    assert D == P and N == 2 * HALF and B % 2 == 0
    TH_ = T // 2

    with ExitStack() as ctx:
        def sb(name, shape, dt=F32):
            return ctx.enter_context(nc.sbuf_tensor(name, shape, dt))

        def sem(name):
            return ctx.enter_context(nc.semaphore(name))

        def sems(name):
            return [sem(f"{name}{s}") for s in range(2)]

        def bufs(name, shape, dt=F32):
            return [sb(f"{name}{s}", shape, dt) for s in range(2)]

        ps = ctx.enter_context(nc.psum_tensor("ps", [P, 8, HALF], F32))

        adj_hi = sb("adj_hi", [P, T, N], F32R)
        adj_lo = sb("adj_lo", [P, T, N], F32R)
        mask = sb("mask", [P, T, N])
        x = bufs("x", [P, T, D])
        xh = bufs("xh", [P, T, D], F32R)
        xl = bufs("xl", [P, T, D], F32R)
        hT = bufs("hT", [P, N])
        th = bufs("th", [P, N], F32R)
        tl = bufs("tl", [P, N], F32R)
        mh = bufs("mh", [P, N], F32R)
        ml = bufs("ml", [P, N], F32R)
        z = bufs("z", [P, N])
        r = sb("r", [P, N])
        v = sb("v", [P, N])
        RING = 3
        ring = [sb(f"ring{i}", [P, N]) for i in range(RING)]
        wh = sb("wh", [P, 12, D], F32R)
        wl = sb("wl", [P, 12, D], F32R)
        w1f = sb("w1f", [P, D])
        we2b = sb("we2b", [P, D])
        ones = sb("ones", [P, P])
        ident = sb("ident", [P, P])
        b0b = sb("b0b", [P, D])
        b1b = sb("b1b", [P, D])
        bmb = sb("bmb", [P, D])
        kb = sb("kb", [P, D])
        sb_bc = sb("sb_bc", [P, 2, P])
        cols = sb("cols", [P, 16])
        wji = cols[:, 0:2]
        we1 = cols[:, 2:3]
        we2 = cols[:, 3:4]
        bi, bn = cols[:, 4:5], cols[:, 5:6]
        w3b, w4b, u3b, w5b, u5b = (cols[:, c:c + 1] for c in range(6, 11))
        wr, gb, be = (cols[:, c:c + 1] for c in range(11, 14))
        zb, rb = cols[:, 14:15], cols[:, 15:16]
        vb = sb("vb", [P, 1])
        sc = bufs("sc", [P, 2])
        sv = bufs("sv", [P, T, 3])
        asrc = bufs("asrc", [P, T])
        st = bufs("st", [P, T, 6])
        mv = bufs("mv", [P, T, 2])
        ve = bufs("ve", [P, T])
        rs = bufs("rs", [P, T])
        mhalf = sb("mhalf", [P, T])

        zflat = [z[s][:, :].rearrange("p (k d) -> p k d", d=D) for s in range(2)]
        rflat = r[:, :].rearrange("p (k d) -> p k d", d=D)
        xflat = [x[s][:, :, :].rearrange("p t d -> p (t d)") for s in range(2)]

        s_w, s_adj = sem("weights_loaded"), [sem(f"adj_loaded{t}") for t in range(T)]
        s_const, s_const0 = sem("consts_set"), sem("consts_zeroed")
        s_comb, s_comb0 = sem("weights_combined"), sem("weight_sums")
        s_wh, s_wl = sem("weight_hi"), sem("weight_lo")
        s_ah, s_al = sem("adj_hi_done"), sem("adj_lo_done")
        s_noedge, s_mask = sem("no_edge_done"), sem("mask_done")
        s_x = sems("x_loaded")
        f_xh, f_xl = sems("f_xh"), sems("f_xl")
        f_xb = sems("f_xb")
        f_m, f_mh, f_ml = sems("f_m"), sems("f_mh"), sems("f_ml")
        f_y, f_sum = sems("f_y"), sems("f_sum")
        f_st = sems("f_st")
        f_mv, f_ve, f_rs, f_xn = sems("f_mv"), sems("f_ve"), sems("f_rs"), sems("f_xn")
        f_p1, f_p2 = sems("f_p1"), sems("f_p2")
        f_t = sems("f_t")
        f_xt = sems("f_xt")
        f_tl = sems("f_tl")
        f_sij, f_svc = sems("f_sij"), sems("f_svc")
        f_s, f_sc, f_k, f_sb = sems("f_s"), sems("f_sc"), sems("f_k"), sems("f_sb")
        f_rw, f_rx, f_kb = sems("f_rw"), sems("f_rx"), sems("f_kb")
        f_g = sems("f_g")
        f_ex, f_em, f_el = sems("f_ex"), sems("f_em"), sems("f_el")
        f_eth = sems("f_eth")
        f_etl = sems("f_etl")
        f_as, f_asb = sems("f_as"), sems("f_asb")
        f_at = sems("f_at")
        f_e, f_ma, f_ag, f_rsum = sems("f_e"), sems("f_ma"), sems("f_ag"), sems("f_rsum")
        f_rb = sems("f_rb")
        f_self, f_sh, f_sl = sems("f_self"), sems("f_sh"), sems("f_sl")
        f_h2r, f_l2r = sems("f_h2r"), sems("f_l2r")
        f_kbx = sems("f_kbx")
        f_h0 = sems("f_h0")
        f_l0 = sems("f_l0")
        m_done, mh_done = sem("m_done"), sem("mh_done")
        z_pre, z_done, r_pre = sem("z_pre"), sem("z_done"), sem("r_pre")
        rh_done, rhh_done = sem("rh_done"), sem("rhh_done")
        v_pre, d_sub, d_mul = sem("v_pre"), sem("d_sub"), sem("d_mul")
        ml_done, r_done, rhl_done = sems("ml_done"), sems("r_done"), sems("rhl_done")
        v_done, h_new = sems("v_done"), sems("h_new")
        t_done, xh_done, xl_done = sems("t_done"), sems("xh_done"), sems("xl_done")
        th_done, tl_done = sems("th_done"), sems("tl_done")
        s_o1, s_o2 = sems("o_first"), sems("o_sum")
        s_out = sems("z_moved")

        def cut(h):
            return slice(h * HALF, (h + 1) * HALF)

        def tile(t):
            return slice(t * P, (t + 1) * P)

        def nat(buf, h):
            return buf[:, h * TH_:(h + 1) * TH_, :]

        def bank(b, h):
            return ps[:, b + h, :]

        def bank4(b, h):
            return ps[:, b + h, :].rearrange("p (t d) -> p t d", d=D)

        block = ctx.enter_context(nc.Block())

        @block.sync
        def _(sp):
            for s, names in enumerate((RAW0, RAW1)):
                for k, name in enumerate(names):
                    sp.dma_start(zflat[s][:, k, :], w[name]).then_inc(
                        s_w if k < len(names) - 1 else s_out[s], 16)
            for s in range(2):
                sp.dma_start(x[s][:, :, :], x_in[s].rearrange("(t p) d -> p t d", p=P)).then_inc(s_x[s], 16)
            for t in range(T):
                sp.dma_start(mask[:, t, :], adjT[tile(t), :]).then_inc(s_adj[t], 16)
            with sp.Fori(0, PAIRS - 1) as p:
                for s in range(2):
                    sp.wait_ge(s_o2[s], p + 1)
                    sp.dma_start(x[s][:, :, :], x_in[p * 2 + 2 + s].rearrange("(t p) d -> p t d", p=P)
                                 ).then_inc(s_x[s], 16)
                for s in range(2):
                    sp.wait_ge(f_xn[s], p * 4 + 4)
                    sp.dma_start(out[p * 2 + s].rearrange("(t p) d -> p t d", p=P), zflat[s]
                                 ).then_inc(s_out[s], 16)
            for s in range(2):
                sp.wait_ge(f_xn[s], PAIRS * 4)
                sp.dma_start(out[B - 2 + s].rearrange("(t p) d -> p t d", p=P), zflat[s]
                             ).then_inc(s_out[s], 16)
            for s in range(2):
                sp.wait_ge(s_out[s], 16 * (PAIRS + 1))

        NCOL = 14
        W_LOADS = len(RAW0) + len(RAW1) - 2 + NCOL + 3

        @block.gpsimd
        def _(pool):
            pool.memset(ones[:, :], 1.0).then_inc(s_const, 1)
            pool.memset(ident[:, :], 0.0).then_inc(s_const0, 1)
            pool.wait_ge(s_const0, 1)
            pool.affine_select(out=ident[:, :], in_=ident[:, :], compare_op=ALU.not_equal, fill=1.0,
                               base=0, pattern=[[-1, P]], channel_multiplier=1).then_inc(s_const, 1)
            pool.memset(mhalf[:, :], -0.5).then_inc(s_const, 1)
            for s in range(2):
                pool.memset(sv[s][:, :, 0:1], 1.0).then_inc(s_const, 1)

            def rstd(s, p, n):
                pool.wait_ge(f_ve[s], p * 4 + n + 1)
                pool.tensor_tensor(rs[s][:, :], ve[s][:, :], mhalf[:, :], ALU.pow).then_inc(f_rs[s], 1)

            pool.wait_ge(s_const, 5)
            pool.wait_ge(s_w, 16 * W_LOADS)
            with pool.Fori(0, PAIRS) as p:
                for s in range(2):
                    pool.wait_ge(f_xl[s], p * 3 + 1)
                    pool.tensor_tensor(x[s][:, :, :], x[s][:, :, :],
                                       b0b[:, :].unsqueeze(1).to_broadcast([P, T, D]), ALU.add).then_inc(f_xb[s], 1)
                for n in range(2):
                    for s in range(2):
                        rstd(s, p, n)
                for s in range(2):
                    pool.wait_ge(f_t[s], p * 8 + 4)
                    pool.tensor_tensor(x[s][:, :, :], x[s][:, :, :],
                                       bmb[:, :].unsqueeze(1).to_broadcast([P, T, D]), ALU.add).then_inc(f_xb[s], 1)
                for s in range(2):
                    if s == 1:
                        pool.wait_ge(f_rb[0], p * 2 + 2)
                    pool.wait_ge(f_el[s], p * 4 + 2)
                    for t in range(T):
                        a, b = r, ring[(s * T + t) % RING]
                        if t == 0:
                            continue
                        if t == 1:
                            a = ring[s * T % RING]
                        else:
                            pool.wait_ge(f_rsum[s], p * (T - 1) + t - 1)
                        pool.wait_ge(f_ma[s], p * T + t + 1)
                        pool.tensor_tensor(r[:, :], a[:, :], b[:, :], ALU.add).then_inc(f_rsum[s], 1)
                for s in range(2):
                    rstd(s, p, 2)
                for s in range(2):
                    rstd(s, p, 3)

        @block.tensor
        def _(pe):
            def adj_product(s, h, inc, each_tile=False):
                for t in range(T):
                    if each_tile:
                        pe.wait_ge(s_al, t + 1)
                    for i, (a, b) in enumerate(((xh, adj_hi), (xh, adj_lo), (xl, adj_hi))):
                        mm = pe.matmul(bank(MB, h), a[s][:, t, :], b[:, t, cut(h)],
                                       start=(t == 0 and i == 0), stop=(t == T - 1 and i == 2))
                mm.then_inc(inc, 1)

            def passes(dst, k, hi, lo, first, last):
                pe.matmul(dst, wh[:, k, :], hi, start=first, stop=False, skip_group_check=True)
                pe.matmul(dst, wl[:, k, :], hi, start=False, stop=False, skip_group_check=True)
                return pe.matmul(dst, wh[:, k, :], lo, start=False, stop=last, skip_group_check=True)

            def to_natural(s, h, parts, inc):
                for j in range(TH_):
                    t = h * TH_ + j
                    dst = ps[:, GB + h, tile(j)]
                    seq = []
                    for hi, lo, k in parts:
                        seq += [(hi, wh, k), (hi, wl, k), (lo, wh, k)]
                    for i, (a, b, k) in enumerate(seq):
                        mm = pe.matmul(dst, a[s][:, tile(t)], b[:, k, :], start=(i == 0),
                                       stop=(i == len(seq) - 1), skip_group_check=True)
                mm.then_inc(inc, 1)

            def turn_nat(s, h, inc):
                for j in range(TH_):
                    mm = pe.transpose(ps[:, TB + h, tile(j)], x[s][:, h * TH_ + j, :], ident[:, :])
                mm.then_inc(inc, 1)

            def turn_T(s, h, inc):
                for j in range(TH_):
                    mm = pe.transpose(ps[:, TB + h, tile(j)], hT[s][:, tile(h * TH_ + j)], ident[:, :])
                mm.then_inc(inc, 1)

            pe.wait_ge(s_const, 5)
            pe.wait_ge(s_wl, 1)

            with pe.Fori(0, PAIRS) as p:
                def layer_m(s, h, n, first=False):
                    if h == 0:
                        pe.wait_ge(f_xl[s], p * 3 + n + 1)
                    if s == 1 or n == 1:
                        pe.wait_ge(f_ml[1 - s], p * 6 + (2 * n if s else 2 * n - 2) + h + 1)
                    adj_product(s, h, f_m[s], each_tile=first)

                def layer_y(s, n, parts, before):
                    for h in range(2):
                        pe.wait_ge(f_ml[s], p * 6 + 2 * n + h + 1)
                        before(h)
                        to_natural(s, h, parts, f_y[s])

                def l1_small(s):
                    pe.wait_ge(f_xt[s], p * 8 + 2)
                    for t in range(T):
                        mm = pe.matmul(ps[:, VB, 2 * t:2 * t + 2], hT[s][:, tile(t)], wji, start=True, stop=True)
                    mm.then_inc(f_sij[s], 1)

                def l1_sums(s):
                    pe.wait_ge(f_svc[s], p + 1)
                    for t in range(T):
                        mm = pe.matmul(ps[:, VB + 1, 0:2], x[s][:, t, :], sv[s][:, t, 0:2],
                                       start=(t == 0), stop=(t == T - 1))
                    mm.then_inc(f_s[s], 1)

                def l1_rows(s):
                    pe.wait_ge(f_sb[s], p * 2 + 2)
                    for i in range(2):
                        mm = pe.matmul(ps[:, VB, tile(i)], sb_bc[:, i, :], w1f[:, :], start=True, stop=True)
                    mm.then_inc(f_rw[s], 1)

                layer_m(0, 0, 0, first=True)
                layer_m(0, 1, 0)
                layer_m(1, 0, 0)
                layer_y(0, 0, [(mh, ml, W0)], lambda h: None)
                layer_m(1, 1, 0)
                layer_y(1, 0, [(mh, ml, W0)], lambda h: pe.wait_ge(f_sum[0], p * 6 + h + 1))

                def l1_turn(s):
                    pe.wait_ge(f_xn[s], p * 4 + 1)
                    if s:
                        pe.wait_ge(f_xt[0], p * 8 + 2)
                        pe.wait_ge(f_kb[0], p + 1)
                        pe.wait_ge(f_rx[0], p + 1)
                    for h in range(2):
                        turn_nat(s, h, f_t[s])

                l1_turn(0)
                layer_m(0, 0, 1)
                l1_small(0)
                layer_m(0, 1, 1)
                l1_sums(0)
                l1_rows(0)
                layer_m(1, 0, 1)
                layer_y(0, 1, [(mh, ml, W1R)], lambda h: pe.wait_ge(f_sum[1], p * 6 + h + 1))
                l1_turn(1)
                l1_small(1)
                layer_m(1, 1, 1)
                l1_sums(1)
                l1_rows(1)
                layer_y(1, 1, [(mh, ml, W1R)], lambda h: pe.wait_ge(f_sum[0], p * 6 + 2 + h + 1))

                for s in range(2):
                    pe.wait_ge(f_xn[s], p * 4 + 2)
                    pe.wait_ge(f_xt[1 - s], p * 8 + (6 if s else 2))
                    for h in range(2):
                        turn_nat(s, h, f_t[s])
                    for h in range(2):
                        pe.wait_ge(f_tl[s], p * 2 + h + 1)
                        if s == 0:
                            pe.wait_ge(f_sum[1], p * 6 + 2 + h + 1)
                        else:
                            pe.wait_ge(f_el[0], p * 4 + h + 1)
                        passes(bank(GB, h), WI, th[s][:, cut(h)], tl[s][:, cut(h)], True, True).then_inc(f_g[s], 1)
                    for h in range(2):
                        pe.wait_ge(f_el[s], p * 4 + h + 1)
                        turn_T(s, h, f_t[s])
                    if s:
                        pe.wait_ge(f_asb[0], p + 1)
                    for t in range(T):
                        mm = pe.matmul(ps[:, VB, t:t + 1], hT[s][:, tile(t)], we1, start=True, stop=True)
                    mm.then_inc(f_as[s], 1)
                for s in range(2):
                    if s == 0:
                        pe.wait_ge(f_el[1], p * 4 + 2)
                    else:
                        pe.wait_ge(f_e[0], p * T + T)
                    for h in range(2):
                        mm = pe.matmul(bank(GB, h), we2b[:, :], hT[s][:, cut(h)], start=True, stop=True)
                    mm.then_inc(f_at[s], 1)
                    if s:
                        pe.wait_ge(f_ml[0], p * 6 + 6)
                    pe.wait_ge(f_xt[s], p * 8 + 6)
                    for t in range(T):
                        pe.wait_ge(f_ma[s], p * T + t + 1)
                        for h in range(2):
                            mm = pe.matmul(bank(MB, h), z[s][:, tile(t)], ring[(s * T + t) % RING][:, cut(h)],
                                           start=(t == 0), stop=(t == T - 1))
                        mm.then_inc(f_ag[s], 1)
                    pe.wait_ge(f_rsum[s], (p + 1) * (T - 1))
                    for h in range(2):
                        if s == 0:
                            pe.wait_ge(f_asb[1], p + 1)
                        else:
                            pe.wait_ge(f_self[0], p * 2 + h + 1)
                        pe.matmul(bank(VB, h), ones[:, :], r[:, cut(h)], start=True, stop=True).then_inc(f_rb[s], 1)
                for s in range(2):
                    for h in range(2):
                        pe.wait_ge(f_ml[s], p * 6 + 4 + h + 1)
                        pe.wait_ge(f_sl[s], p * 2 + h + 1)
                        if s == 0:
                            pe.wait_ge(f_e[1], p * T + T)
                        else:
                            pe.wait_ge(f_sum[0], p * 6 + 4 + h + 1)
                        passes(bank(GB, h), WNA, mh[s][:, cut(h)], ml[s][:, cut(h)], True, False)
                        passes(bank(GB, h), WNB, xh[s][:, h * TH_:(h + 1) * TH_, :].rearrange("p t d -> p (t d)"),
                               xl[s][:, h * TH_:(h + 1) * TH_, :].rearrange("p t d -> p (t d)"), False, True
                               ).then_inc(f_g[s], 1)
                    for h in range(2):
                        pe.wait_ge(f_l2r[s], p * 2 + h + 1)
                        to_natural(s, h, [(mh, ml, WMA), (th, tl, WMB)], f_y[s])
                for s in range(2):
                    pe.wait_ge(f_xn[s], p * 4 + 3)
                    if s:
                        pe.wait_ge(f_xt[0], p * 8 + 8)
                    for h in range(2):
                        turn_nat(s, h, f_t[s])

                def candidate(s, k):
                    for h in range(2):
                        pe.wait_ge(rhl_done[s], k * 2 + h + 1)
                        pre_v(s, h, k)
                        passes(bank(VB, h), U5, th[s][:, cut(h)], tl[s][:, cut(h)], True, False)
                        passes(bank(VB, h), W5, mh[s][:, cut(h)], ml[s][:, cut(h)], False, True
                               ).then_inc(v_pre, 1)

                def pre_v(s, h, k):
                    if s == 1:
                        pe.wait_ge(v_done[0], k * 2 + h + 1)
                    elif first_step[0]:
                        pe.wait_ge(f_self[1], p * 2 + h + 1)
                    else:
                        pe.wait_ge(v_done[1], k * 2 + h - 1)

                def turn_state(s, k):
                    for h in range(2):
                        pe.wait_ge(h_new[s], k * 2 + h + 1)
                        if s == 1:
                            pe.wait_ge(xl_done[0], k * 2 + h + 1)
                        elif first_step[0]:
                            pe.wait_ge(f_xt[1], p * 8 + 8)
                        else:
                            pe.wait_ge(xl_done[1], k * 2 + h - 1)
                        turn_T(s, h, t_done[s])

                first_step = [False]

                def gates(s, k, first, i):
                    if first:
                        pe.wait_ge(f_l0[s], p + 1)
                    else:
                        pe.wait_ge(tl_done[s], p * (STEPS - 1) + i if s else k)
                    for h in range(2):
                        if s == 1:
                            pe.wait_ge(r_done[0], k * 2 + h + 1)
                        elif first:
                            pe.wait_ge(f_sum[1], p * 6 + 4 + h + 1)
                        else:
                            pe.wait_ge(r_done[1], k * 2 + h - 1)
                        passes(bank(GB, h), U3, th[s][:, cut(h)], tl[s][:, cut(h)], True, False)
                    for h in range(2):
                        pe.wait_ge(ml_done[s], k * 2 + h + 1)
                        passes(bank(GB, h), W3, mh[s][:, cut(h)], ml[s][:, cut(h)], False, True
                               ).then_inc(z_pre, 1)
                    for h in range(2):
                        pe.wait_ge(z_done, k * 4 + 2 * s + h + 1)
                        passes(bank(GB, h), WD, mh[s][:, cut(h)], ml[s][:, cut(h)], False, True
                               ).then_inc(r_pre, 1)

                def state_product(s, h, k, first):
                    if h == 0:
                        if first:
                            pe.wait_ge(f_xl[s], p * 3 + 3)
                        else:
                            pe.wait_ge(xl_done[s], k * 2)
                    if s == 1:
                        pe.wait_ge(ml_done[0], k * 2 + h + 1)
                    elif first:
                        pe.wait_ge(f_ml[1], p * 6 + 4 + h + 1)
                    else:
                        pe.wait_ge(ml_done[1], k * 2 + h - 1)
                    adj_product(s, h, m_done)

                def step(k, first, i=0):
                    first_step[0] = first
                    state_product(0, 0, k, first)
                    if not first:
                        candidate(1, k - 1)
                    state_product(0, 1, k, first)
                    if not first:
                        turn_state(1, k - 1)
                    gates(0, k, first, i)
                    state_product(1, 0, k, first)
                    candidate(0, k)
                    state_product(1, 1, k, first)
                    turn_state(0, k)
                    gates(1, k, first, i)

                step(pe.snap(p * STEPS), True)
                with pe.Fori(1, STEPS) as i:
                    step(pe.snap(p * STEPS + i), False, i)
                last = pe.snap(p * STEPS + STEPS - 1)
                candidate(1, last)
                turn_state(1, last)
                pe.wait_ge(xl_done[1], last * 2 + 2)

        @block.scalar
        def _(act):
            vecs = [("wj", 0), ("wi", 1), ("we1", 2), ("we2", 3), ("bi", 4), ("bn", 5), ("w3_b", 6),
                    ("w4_b", 7), ("u3_b", 8), ("w5_b", 9), ("u5_b", 10)]
            for name, c in vecs:
                act.dma_start(cols[:, c:c + 1], w[name]).then_inc(s_w, 16)
            for name, c in (("wr", 11), ("gb", 12), ("be", 13)):
                act.dma_start(cols[:, c:c + 1], w[name].to_broadcast([P, 1])).then_inc(s_w, 16)
            for name, t in (("b0", b0b), ("b1", b1b), ("bm", bmb)):
                act.dma_start(t[:, :], w[name].to_broadcast([P, D])).then_inc(s_w, 16)

            def copy(dst, src):
                return act.activation(dst, src, ACT.Copy)

            act.wait_ge(s_comb, 1)
            copy(wh[:, 0:8, :], ring[0][:, :].rearrange("p (k d) -> p k d", d=D)).then_inc(s_wh, 1)
            copy(wh[:, 8:12, :], ring[1][:, 0:4 * D].rearrange("p (k d) -> p k d", d=D)).then_inc(s_wh, 1)
            for t in range(T):
                act.wait_ge(s_adj[t], 16)
                copy(adj_hi[:, t, :], mask[:, t, :]).then_inc(s_ah, 1)

            with act.Fori(0, PAIRS) as p:
                def m_hi(s, n):
                    for h in range(2):
                        if n < 2:
                            act.wait_ge(f_m[s], p * 4 + 2 * n + h + 1)
                        else:
                            act.wait_ge(f_ag[s], p * T + T)
                        copy(mh[s][:, cut(h)], bank(MB, h)).then_inc(f_mh[s], 1)

                def x_hi(s, n, ready):
                    ready()
                    copy(xh[s][:, :, :], x[s][:, :, :]).then_inc(f_xh[s], 1)

                for s in range(2):
                    x_hi(s, 0, lambda: act.wait_ge(s_x[s], p * 16 + 16))
                for s in range(2):
                    m_hi(s, 0)

                def l1_head(s):
                    x_hi(s, 1, lambda: act.wait_ge(f_xn[s], p * 4 + 1))
                    for h in range(2):
                        act.wait_ge(f_t[s], p * 8 + h + 1)
                        copy(hT[s][:, cut(h)], bank(TB, h)).then_inc(f_xt[s], 1)

                l1_head(0)
                m_hi(0, 1)
                l1_head(1)
                m_hi(1, 1)

                def elu_exp(s, n, b):
                    for h in range(2):
                        act.wait_ge(f_g[s], p * 4 + 2 * n + h + 1)
                        if h == 0 and n == 0 and s == 1:
                            act.wait_ge(f_el[0], p * 4 + 2)
                        if h == 0 and n == 1:
                            act.wait_ge(f_rb[1], p * 2 + 2)
                            if s == 1:
                                act.wait_ge(f_el[0], p * 4 + 4)
                        act.activation(r[:, cut(h)], bank(GB, h), ACT.Exp, bias=b).then_inc(f_ex[s], 1)

                for s in range(2):
                    for h in range(2):
                        act.wait_ge(f_t[s], p * 8 + 2 + h + 1)
                        copy(th[s][:, cut(h)], bank(TB, h)).then_inc(f_xt[s], 1)
                    elu_exp(s, 0, bi)
                    act.wait_ge(s_out[s], p * 16 + 16)
                    for h in range(2):
                        act.wait_ge(f_t[s], p * 8 + 4 + h + 1)
                        copy(z[s][:, cut(h)], bank(TB, h)).then_inc(f_xt[s], 1)
                    for h in range(2):
                        copy(th[s][:, cut(h)], hT[s][:, cut(h)]).then_inc(f_eth[s], 1)
                for s in range(2):
                    act.wait_ge(f_at[s], p + 1)
                    act.wait_ge(f_asb[s], p + 1)
                    for t in range(T):
                        u = s * T + t
                        if u >= RING:
                            q, o = divmod(u - RING, T)
                            act.wait_ge(f_ag[q], p * T + o + 1)
                            act.wait_ge(f_rsum[q], p * (T - 1) + max(o, 1))
                        act.activation(ring[u % RING][:, :].rearrange("p (h n) -> p h n", h=2), ps[:, GB:GB + 2, :],
                                       ACT.Sigmoid, bias=asrc[s][:, t:t + 1]).then_inc(f_e[s], 1)
                    for h in range(2):
                        act.wait_ge(f_self[s], p * 2 + h + 1)
                        copy(xh[s][:, h * TH_:(h + 1) * TH_, :].rearrange("p t d -> p (t d)"), v[:, cut(h)]
                             ).then_inc(f_sh[s], 1)
                    m_hi(s, 2)
                for s in range(2):
                    elu_exp(s, 1, bn)
                    for h in range(2):
                        act.wait_ge(f_el[s], p * 4 + 2 + h + 1)
                        copy(mh[s][:, cut(h)], hT[s][:, cut(h)]).then_inc(f_h2r[s], 1)
                for s in range(2):
                    x_hi(s, 2, lambda: act.wait_ge(f_xn[s], p * 4 + 3))
                    for h in range(2):
                        act.wait_ge(f_t[s], p * 8 + 6 + h + 1)
                        copy(hT[s][:, cut(h)], bank(TB, h)).then_inc(f_xt[s], 1)
                    for h in range(2):
                        act.wait_ge(f_xt[s], p * 8 + 6 + h + 1)
                        copy(th[s][:, cut(h)], hT[s][:, cut(h)]).then_inc(f_h0[s], 1)

                def m_split(s, h, k):
                    act.wait_ge(m_done, k * 4 + 2 * s + h + 1)
                    copy(mh[s][:, cut(h)], bank(MB, h)).then_inc(mh_done, 1)

                def reset_hi(s, k):
                    for h in range(2):
                        act.wait_ge(rh_done, k * 4 + 2 * s + h + 1)
                        copy(th[s][:, cut(h)], r[:, cut(h)]).then_inc(rhh_done, 1)

                def candidate(s, k):
                    for h in range(2):
                        act.wait_ge(v_pre, k * 4 + 2 * s + h + 1)
                        if s == 1:
                            act.wait_ge(h_new[0], k * 2 + h + 1)
                        elif not first_step[0]:
                            act.wait_ge(h_new[1], k * 2 + h - 1)
                        act.activation(v[:, cut(h)], bank(VB, h), ACT.Tanh, bias=vb[:, :]).then_inc(v_done[s], 1)

                def state_hi(s, k):
                    for h in range(2):
                        act.wait_ge(t_done[s], k * 2 + h + 1)
                        copy(nat(xh[s], h), bank4(TB, h)).then_inc(xh_done[s], 1)

                def gates(s, k):
                    for h in range(2):
                        act.wait_ge(z_pre, k * 4 + 2 * s + h + 1)
                        act.activation(z[s][:, cut(h)], bank(GB, h), ACT.Sigmoid, bias=zb).then_inc(z_done, 1)
                    for h in range(2):
                        act.wait_ge(r_pre, k * 4 + 2 * s + h + 1)
                        if s == 1:
                            act.wait_ge(rhl_done[0], k * 2 + h + 1)
                        elif not first_step[0]:
                            act.wait_ge(rhl_done[1], k * 2 + h - 1)
                        act.activation(r[:, cut(h)], bank(GB, h), ACT.Sigmoid, bias=rb).then_inc(r_done[s], 1)

                def turned_hi(s, k):
                    act.wait_ge(h_new[s], k * 2 + 2)
                    copy(th[s][:, :], hT[s][:, :]).then_inc(th_done[s], 1)

                first_step = [False]

                def step(k, first, i=0):
                    first_step[0] = first
                    if not first:
                        reset_hi(1, k - 1)
                    m_split(0, 0, k)
                    if not first:
                        candidate(1, k - 1)
                    m_split(0, 1, k)
                    if not first:
                        state_hi(1, k - 1)
                    gates(0, k)
                    if not first:
                        turned_hi(1, k - 1)
                    reset_hi(0, k)
                    m_split(1, 0, k)
                    candidate(0, k)
                    m_split(1, 1, k)
                    state_hi(0, k)
                    gates(1, k)
                    turned_hi(0, k)

                step(act.snap(p * STEPS), True)
                with act.Fori(1, STEPS) as i:
                    step(act.snap(p * STEPS + i), False, i)
                last = act.snap(p * STEPS + STEPS - 1)
                reset_hi(1, last)
                candidate(1, last)
                state_hi(1, last)
                act.wait_ge(t_done[1], last * 2 + 2)
                for s in range(2):
                    act.wait_ge(s_o2[s], p + 1)

        @block.vector
        def _(dve):
            dve.wait_ge(s_w, 16 * W_LOADS)
            for s in range(2):
                dve.wait_ge(s_out[s], 16)
            cf = [ring[i][:, :].rearrange("p (k d) -> p k d", d=D) for i in range(2)]
            dve.tensor_copy(ring[0][:, :], z[0][:, :]).then_inc(s_comb0, 1)
            dve.tensor_copy(w1f[:, :], zflat[0][:, 1, :]).then_inc(s_comb0, 1)
            dve.tensor_tensor(cf[1][:, 0, :], zflat[1][:, 0, :], zflat[1][:, 1, :], ALU.add).then_inc(s_comb0, 1)
            dve.tensor_tensor(rflat[:, 0, :], zflat[1][:, 2, :], zflat[1][:, 3, :], ALU.add).then_inc(s_comb0, 1)
            dve.tensor_tensor(cf[1][:, 2, :], zflat[1][:, 4, :], zflat[1][:, 5, :], ALU.add).then_inc(s_comb0, 1)
            dve.tensor_copy(cf[1][:, 3, :], zflat[1][:, 6, :]).then_inc(s_comb0, 1)
            dve.tensor_tensor(zb, w3b, u3b, ALU.add).then_inc(s_comb0, 1)
            dve.tensor_tensor(rb, w4b, u3b, ALU.add).then_inc(s_comb0, 1)
            dve.tensor_tensor(vb[:, :], w5b, u5b, ALU.add).then_inc(s_comb0, 1)
            dve.wait_ge(s_const, 5)
            dve.tensor_scalar(we2b[:, :], ones[:, :], we2, None, ALU.mult).then_inc(s_comb0, 1)
            dve.wait_ge(s_comb0, 10)
            dve.tensor_scalar(cf[0][:, W1R, :], w1f[:, :], wr, None, ALU.mult).then_inc(s_comb0, 1)
            dve.tensor_tensor(cf[1][:, 1, :], rflat[:, 0, :], cf[1][:, 0, :], ALU.subtract).then_inc(s_comb0, 1)
            dve.wait_ge(s_comb0, 12)
            dve.memset(kb[:, :], 0.0).then_inc(s_comb, 1)
            dve.wait_ge(s_wh, 2)
            dve.tensor_tensor(wl[:, 0:8, :], cf[0], wh[:, 0:8, :].bitcast(F32), ALU.subtract)
            dve.tensor_tensor(wl[:, 8:12, :], cf[1][:, 0:4, :], wh[:, 8:12, :].bitcast(F32), ALU.subtract
                              ).then_inc(s_wl, 1)
            for t in range(T):
                dve.wait_ge(s_ah, t + 1)
                dve.tensor_tensor(adj_lo[:, t, :], mask[:, t, :], adj_hi[:, t, :].bitcast(F32), ALU.subtract
                                  ).then_inc(s_al, 1)
            dve.wait_ge(s_wl, 1)
            for t in range(T):
                if t >= 2:
                    dve.wait_ge(s_mask, t - 1)
                dve.tensor_scalar(ring[t % 2][:, :], mask[:, t, :], 0.0, ALPHA, ALU.is_equal, ALU.mult
                                  ).then_inc(s_noedge, 1)
                dve.wait_ge(s_noedge, t + 1)
                dve.wait_ge(s_al, t + 1)
                dve.tensor_tensor(mask[:, t, :], mask[:, t, :], ring[t % 2][:, :], ALU.add).then_inc(s_mask, 1)
            dve.wait_ge(s_mask, T)

            def lo(dst, src, hi):
                return dve.tensor_tensor(dst, src, hi.bitcast(F32), ALU.subtract)

            with dve.Fori(0, PAIRS) as p:
                def m_lo(s, n):
                    for h in range(2):
                        dve.wait_ge(f_mh[s], p * 6 + 2 * n + h + 1)
                        lo(ml[s][:, cut(h)], bank(MB, h), mh[s][:, cut(h)]).then_inc(f_ml[s], 1)

                def x_lo(s, n):
                    dve.wait_ge(f_xh[s], p * 3 + n + 1)
                    lo(xl[s][:, :, :], x[s][:, :, :], xh[s][:, :, :]).then_inc(f_xl[s], 1)

                def norm_stats(s, n, src):
                    for t in range(T):
                        ins = dve.bn_stats(st[s][:, t, :], src[:, t, :])
                    ins.then_inc(f_st[s], 1)
                    m_e, m_o, q_e, q_o = (st[s][:, :, c] for c in (1, 4, 2, 5))
                    dve.wait_ge(f_st[s], p * 4 + n + 1)
                    dve.tensor_tensor(mv[s][:, :, 0], m_e, m_o, ALU.add).then_inc(f_p1[s], 1)
                    dve.tensor_tensor(mv[s][:, :, 1], m_e, m_o, ALU.subtract).then_inc(f_p1[s], 1)
                    dve.tensor_tensor(ve[s][:, :], q_e, q_o, ALU.add).then_inc(f_p1[s], 1)
                    dve.wait_ge(f_p1[s], p * 12 + n * 3 + 3)
                    dve.scalar_tensor_tensor(out=mv[s][:, :, 1], in0=mv[s][:, :, 1], scalar=0.25,
                                             in1=mv[s][:, :, 1], op0=ALU.mult, op1=ALU.mult).then_inc(f_p2[s], 1)
                    dve.tensor_scalar(ve[s][:, :], ve[s][:, :], 1.0 / D, EPS, ALU.mult, ALU.add).then_inc(f_p2[s], 1)
                    dve.tensor_scalar(mv[s][:, :, 0], mv[s][:, :, 0], 0.5, None, ALU.mult).then_inc(f_mv[s], 1)
                    dve.wait_ge(f_p2[s], p * 8 + n * 2 + 2)
                    dve.tensor_tensor(ve[s][:, :], ve[s][:, :], mv[s][:, :, 1], ALU.add).then_inc(f_ve[s], 1)

                def norm_apply(s, n, dst, src):
                    dve.wait_ge(f_rs[s], p * 4 + n + 1)
                    dve.wait_ge(f_mv[s], p * 4 + n + 1)
                    for t in range(T):
                        ins = dve.tensor_scalar(dst[:, t, :], src[:, t, :], mv[s][:, t, 0:1], rs[s][:, t:t + 1],
                                                ALU.subtract, ALU.mult)
                    ins.then_inc(f_xn[s], 1)

                def layer_out(s, n, ready):
                    ready()
                    for h in range(2):
                        dve.wait_ge(f_y[s], p * 6 + 2 * n + h + 1)
                        dve.tensor_tensor(nat(x[s], h), bank4(GB, h), nat(x[s], h), ALU.add).then_inc(f_sum[s], 1)
                    dve.wait_ge(f_sum[s], p * 6 + 2 * n + 2)
                    norm_stats(s, n, x[s])

                for s in range(2):
                    x_lo(s, 0)
                m_lo(0, 0)
                layer_out(0, 0, lambda: dve.wait_ge(f_xb[0], p * 2 + 1))
                norm_apply(0, 0, x[0], x[0])
                dve.wait_ge(f_xn[0], p * 4 + 1)
                x_lo(0, 1)
                m_lo(1, 0)
                layer_out(1, 0, lambda: dve.wait_ge(f_xb[1], p * 2 + 1))
                norm_apply(1, 0, x[1], x[1])

                def l1_vectors(s):
                    dve.wait_ge(f_sij[s], p + 1)
                    dve.tensor_copy(sv[s][:, :, 1:3], ps[:, VB, 0:2 * T].rearrange("p (t c) -> p t c", c=2)
                                    ).then_inc(f_svc[s], 1)

                def l1_consts(s):
                    dve.wait_ge(f_s[s], p + 1)
                    dve.tensor_copy(sc[s][:, :], ps[:, VB + 1, 0:2]).then_inc(f_sc[s], 1)
                    dve.wait_ge(f_sc[s], p + 1)
                    dve.scalar_tensor_tensor(out=sc[s][:, 1:2], in0=sc[s][:, 0:1], scalar=gb, in1=sc[s][:, 1:2],
                                             op0=ALU.mult, op1=ALU.add).then_inc(f_k[s], 1)
                    dve.wait_ge(f_k[s], p + 1)
                    for i in range(2):
                        dve.tensor_scalar(sb_bc[:, i, :], ones[:, :], sc[s][:, i:i + 1], None, ALU.mult
                                          ).then_inc(f_sb[s], 1)

                def l1_residual(s):
                    dve.wait_ge(f_rw[s], p + 1)
                    dve.wait_ge(f_xl[s], p * 3 + 2)
                    for t in range(T):
                        ins = dve.scalar_tensor_tensor(out=x[s][:, t, :], in0=ps[:, VB, 0:P],
                                                       scalar=sv[s][:, t, 2:3], in1=x[s][:, t, :],
                                                       op0=ALU.mult, op1=ALU.add)
                    ins.then_inc(f_rx[s], 1)
                    dve.tensor_tensor(kb[:, :], ps[:, VB, P:2 * P], b1b[:, :], ALU.add).then_inc(f_kb[s], 1)
                    dve.wait_ge(f_kb[s], p + 1)
                    dve.wait_ge(f_rx[s], p + 1)
                    dve.tensor_tensor(x[s][:, :, :], x[s][:, :, :], kb[:, :].unsqueeze(1).to_broadcast([P, T, D]),
                                      ALU.add).then_inc(f_kbx[s], 1)

                l1_vectors(0)
                dve.wait_ge(f_xn[1], p * 4 + 1)
                x_lo(1, 1)
                l1_consts(0)
                m_lo(0, 1)
                l1_residual(0)
                layer_out(0, 1, lambda: dve.wait_ge(f_kbx[0], p + 1))
                norm_apply(0, 1, x[0], x[0])
                l1_vectors(1)
                l1_consts(1)
                m_lo(1, 1)
                l1_residual(1)
                layer_out(1, 1, lambda: dve.wait_ge(f_kbx[1], p + 1))
                norm_apply(1, 1, x[1], x[1])

                def elu(s, n, b):
                    for h in range(2):
                        dve.wait_ge(f_ex[s], p * 4 + 2 * n + h + 1)
                        dve.tensor_scalar(r[:, cut(h)], r[:, cut(h)], 1.0, 1.0, ALU.min, ALU.subtract
                                          ).then_inc(f_em[s], 1)
                        dve.wait_ge(f_em[s], p * 4 + 2 * n + h + 1)
                        dve.scalar_tensor_tensor(out=hT[s][:, cut(h)], in0=bank(GB, h), scalar=b, in1=r[:, cut(h)],
                                                 op0=ALU.add, op1=ALU.max).then_inc(f_el[s], 1)

                for s in range(2):
                    for h in range(2):
                        dve.wait_ge(f_xt[s], p * 8 + 2 + h + 1)
                        lo(tl[s][:, cut(h)], bank(TB, h), th[s][:, cut(h)]).then_inc(f_tl[s], 1)
                    elu(s, 0, bi)
                    dve.wait_ge(f_as[s], p + 1)
                    dve.tensor_scalar(asrc[s][:, :], ps[:, VB, 0:T], be, None, ALU.add).then_inc(f_asb[s], 1)
                    for h in range(2):
                        dve.wait_ge(f_eth[s], p * 2 + h + 1)
                        lo(tl[s][:, cut(h)], hT[s][:, cut(h)], th[s][:, cut(h)]).then_inc(f_etl[s], 1)
                for s in range(2):
                    for t in range(T):
                        u = s * T + t
                        dve.wait_ge(f_e[s], p * T + t + 1)
                        dve.tensor_tensor(ring[u % RING][:, :], ring[u % RING][:, :], mask[:, t, :], ALU.mult
                                          ).then_inc(f_ma[s], 1)
                    for h in range(2):
                        dve.wait_ge(f_rb[s], p * 2 + h + 1)
                        if s == 1:
                            dve.wait_ge(f_sl[0], p * 2 + h + 1)
                        dve.tensor_tensor(v[:, cut(h)], bank(VB, h), hT[s][:, cut(h)], ALU.mult
                                          ).then_inc(f_self[s], 1)
                    for h in range(2):
                        dve.wait_ge(f_sh[s], p * 2 + h + 1)
                        lo(xl[s][:, h * TH_:(h + 1) * TH_, :].rearrange("p t d -> p (t d)"), v[:, cut(h)],
                           xh[s][:, h * TH_:(h + 1) * TH_, :].rearrange("p t d -> p (t d)")).then_inc(f_sl[s], 1)
                    m_lo(s, 2)
                for s in range(2):
                    elu(s, 1, bn)
                    for h in range(2):
                        dve.wait_ge(f_h2r[s], p * 2 + h + 1)
                        lo(ml[s][:, cut(h)], hT[s][:, cut(h)], mh[s][:, cut(h)]).then_inc(f_l2r[s], 1)
                    layer_out(s, 2, lambda: dve.wait_ge(f_xb[s], p * 2 + 2))
                    norm_apply(s, 2, x[s], x[s])
                for s in range(2):
                    dve.wait_ge(f_xn[s], p * 4 + 3)
                    x_lo(s, 2)
                    dve.wait_ge(f_h0[s], p * 2 + 2)
                    lo(tl[s][:, :], hT[s][:, :], th[s][:, :]).then_inc(f_l0[s], 1)

                def m_split(s, h, k):
                    dve.wait_ge(mh_done, k * 4 + 2 * s + h + 1)
                    lo(ml[s][:, cut(h)], bank(MB, h), mh[s][:, cut(h)]).then_inc(ml_done[s], 1)

                def reset(s, k):
                    for h in range(2):
                        dve.wait_ge(r_done[s], k * 2 + h + 1)
                        dve.tensor_tensor(r[:, cut(h)], r[:, cut(h)], hT[s][:, cut(h)], ALU.mult
                                          ).then_inc(rh_done, 1)

                def reset_lo(s, k):
                    for h in range(2):
                        dve.wait_ge(rhh_done, k * 4 + 2 * s + h + 1)
                        lo(tl[s][:, cut(h)], r[:, cut(h)], th[s][:, cut(h)]).then_inc(rhl_done[s], 1)

                def update(s, k):
                    for h in range(2):
                        dve.wait_ge(v_done[s], k * 2 + h + 1)
                        dve.tensor_tensor(v[:, cut(h)], v[:, cut(h)], hT[s][:, cut(h)], ALU.subtract
                                          ).then_inc(d_sub, 1)
                        dve.wait_ge(d_sub, k * 4 + 2 * s + h + 1)
                        dve.tensor_tensor(v[:, cut(h)], v[:, cut(h)], z[s][:, cut(h)], ALU.mult
                                          ).then_inc(d_mul, 1)
                        dve.wait_ge(d_mul, k * 4 + 2 * s + h + 1)
                        dve.tensor_tensor(hT[s][:, cut(h)], hT[s][:, cut(h)], v[:, cut(h)], ALU.add
                                          ).then_inc(h_new[s], 1)

                def state_lo(s, k):
                    for h in range(2):
                        dve.wait_ge(xh_done[s], k * 2 + h + 1)
                        lo(nat(xl[s], h), bank4(TB, h), nat(xh[s], h)).then_inc(xl_done[s], 1)

                def turned_lo(s, k, i=0):
                    dve.wait_ge(th_done[s], p * (STEPS - 1) + i if s else k + 1)
                    lo(tl[s][:, :], hT[s][:, :], th[s][:, :]).then_inc(tl_done[s], 1)

                def step(k, first, i=0):
                    if not first:
                        reset(1, k - 1)
                        turned_lo(0, k - 1)
                        reset_lo(1, k - 1)
                    m_split(0, 0, k)
                    if not first:
                        update(1, k - 1)
                    m_split(0, 1, k)
                    if not first:
                        state_lo(1, k - 1)
                    reset(0, k)
                    if not first:
                        turned_lo(1, k - 1, i)
                    reset_lo(0, k)
                    m_split(1, 0, k)
                    update(0, k)
                    m_split(1, 1, k)
                    state_lo(0, k)

                step(dve.snap(p * STEPS), True)
                with dve.Fori(1, STEPS) as i:
                    step(dve.snap(p * STEPS + i), False, i)
                last = dve.snap(p * STEPS + STEPS - 1)

                def output(s):
                    dve.wait_ge(xl_done[s], last * 2 + 2)
                    dve.tensor_tensor(zflat[s], x[s][:, :, :], xh[s][:, :, :].bitcast(F32), ALU.add).then_inc(s_o1[s], 1)
                    dve.wait_ge(s_o1[s], p + 1)
                    dve.tensor_tensor(zflat[s], zflat[s], xl[s][:, :, :].bitcast(F32), ALU.add).then_inc(s_o2[s], 1)
                    dve.wait_ge(s_o2[s], p + 1)
                    norm_stats(s, 3, zflat[s])
                    norm_apply(s, 3, zflat[s], zflat[s])

                reset(1, last)
                turned_lo(0, last)
                reset_lo(1, last)
                update(1, last)
                output(0)
                state_lo(1, last)
                output(1)
                dve.wait_ge(t_done[1], last * 2 + 2)


def kernel(**inputs):
    import numpy as _np
    import concourse.bacc as _bacc
    from concourse import mybir as _mybir
    from concourse.bass_utils import run_bass_kernel_spmd as _run

    a = {k: _np.asarray(v) for k, v in inputs.items()}
    D = a["x"].shape[2]
    lay = {
        "x": a["x"], "adjT": a["adj"].T,
        "W0": a["L0_gnn_weight"], "b0": a["L0_gnn_bias"].reshape(1, D),
        "wj": a["L1_gnn_g_w"][:D].reshape(D, 1), "wi": a["L1_gnn_g_w"][D:2 * D].reshape(D, 1),
        "wr": a["L1_gnn_g_w"][2 * D:].reshape(1, 1), "gb": a["L1_gnn_g_b"].reshape(1, 1),
        "W1": a["L1_gnn_weight"], "b1": a["L1_gnn_bias"].reshape(1, D),
        "Wi": a["L2_gnn_Wi"], "bi": a["L2_gnn_bi"].reshape(D, 1),
        "we1": a["L2_gnn_We"][:D], "we2": a["L2_gnn_We"][D:], "be": a["L2_gnn_be"].reshape(1, 1),
        "WnA": a["L2_gnn_Wn"][:D], "WnB": a["L2_gnn_Wn"][D:], "bn": a["L2_gnn_bn"].reshape(D, 1),
        "WmA": a["L2_gnn_Wm"][:D], "WmB": a["L2_gnn_Wm"][D:], "bm": a["L2_gnn_bm"].reshape(1, D),
        "w3a": a["L3_gnn_w3_w"][:, :D].T, "w3b": a["L3_gnn_w3_w"][:, D:].T,
        "w4a": a["L3_gnn_w4_w"][:, :D].T, "w4b": a["L3_gnn_w4_w"][:, D:].T,
        "w5a": a["L3_gnn_w5_w"][:, :D].T, "w5b": a["L3_gnn_w5_w"][:, D:].T,
        "u3": a["L3_gnn_u3_w"].T, "u5": a["L3_gnn_u5_w"].T,
        "w3_b": a["L3_gnn_w3_b"].reshape(D, 1), "w4_b": a["L3_gnn_w4_b"].reshape(D, 1),
        "w5_b": a["L3_gnn_w5_b"].reshape(D, 1), "u3_b": a["L3_gnn_u3_b"].reshape(D, 1),
        "u5_b": a["L3_gnn_u5_b"].reshape(D, 1),
    }
    nc = _bacc.Bacc("TRN2", target_bir_lowering=False, num_devices=1)
    arrays, aps = {}, {}
    for name, v in lay.items():
        v = _np.ascontiguousarray(v)
        arrays[f"in_{name}"] = v
        aps[name] = nc.dram_tensor(f"in_{name}", v.shape, _mybir.dt.from_np(v.dtype), kind="ExternalInput").ap()
    out = nc.dram_tensor("out", a["x"].shape, _mybir.dt.from_np(a["x"].dtype), kind="ExternalOutput").ap()
    program(nc, aps["x"], aps["adjT"], aps, out)
    res = _run(nc, [arrays], core_ids=[0])
    return res.results[0]["out"]
```

```python
from contextlib import ExitStack

import concourse.bass as bass
from concourse import mybir

P = 128
HALF = 512
ALPHA = 0.005
EPS = 1e-5
STEPS = 5

ALU = mybir.AluOpType
ACT = mybir.ActivationFunctionType
F32 = mybir.dt.float32
F32R = mybir.dt.float32r

(U3, W3, WD, W5, U5) = range(5)
(W0, W1R, WI, WNA, WNB, WMA, WMB) = range(7)
RAW0 = ["W0", "W1", "Wi", "WnA", "WnB", "WmA", "WmB", "u3"]
RAW1 = ["w3a", "w3b", "w4a", "w4b", "w5a", "w5b", "u5"]
FB, MB, TB, GB, VB = 0, 2, 3, 4, 6
BATCH = ["x0", "m0a", "m0b", "", "y0", "v0", "n0", "", "m1a", "m1b", "sums", "rows", "y1", "v1", "n1",
         "turn2", "", "proj", "", "turnh", "target s0", "s1", "e0 s2", "e1 s3", "e2 s4", "e3 s5", "e4 s6",
         "e5 s7", "e6", "e7", "", "rowsum", "", "recv", "", "y2", "v2", "n2"]


def program(nc, x_in, adjT, w, mask_dram, out):
    B, N, D = x_in.shape
    T = N // P
    PAIRS = B // 2
    LAST = PAIRS - 1
    assert D == P and N == 2 * HALF and B % 2 == 0
    HT = T // 2

    with ExitStack() as ctx:
        def sb(name, shape, dt=F32):
            return ctx.enter_context(nc.sbuf_tensor(name, shape, dt))

        def sem(name):
            return ctx.enter_context(nc.semaphore(name))

        def sems(name):
            return [sem(f"{name}{s}") for s in range(2)]

        def bufs(name, shape, dt=F32):
            return [sb(f"{name}{s}", shape, dt) for s in range(2)]

        ps = ctx.enter_context(nc.psum_tensor("ps", [P, 8, HALF], F32))

        adj_hi = sb("adj_hi", [P, T, N], F32R)
        adj_lo = sb("adj_lo", [P, T, N], F32R)
        x = bufs("x", [P, T, D])
        xh = bufs("xh", [P, T, D], F32R)
        xl = bufs("xl", [P, T, D], F32R)
        hT = bufs("hT", [P, N])
        th = bufs("th", [P, N], F32R)
        tl = bufs("tl", [P, N], F32R)
        z = bufs("z", [P, N])
        mh = sb("mh", [P, N], F32R)
        ml = sb("ml", [P, N], F32R)
        r = sb("r", [P, N])
        v = sb("v", [P, N])
        xf = bufs("xf", [P, T, D])
        fxh = sb("fxh", [P, T, D], F32R)
        fxl = sb("fxl", [P, T, D], F32R)
        fm = sb("fm", [P, N])
        fh = sb("fh", [P, N])
        fz = sb("fz", [P, N])
        fr = sb("fr", [P, N])
        fv = sb("fv", [P, N])
        ring = [sb(f"ring{i}", [P, N]) for i in range(3)]
        mk = [sb(f"mk{i}", [P, N]) for i in range(2)]

        wh = sb("wh", [P, 5, D], F32R)
        wl = sb("wl", [P, 5, D], F32R)
        wf = sb("wf", [P, 7, D])
        w1f = sb("w1f", [P, D])
        we2b = sb("we2b", [P, D])
        ones = sb("ones", [P, P])
        ident = sb("ident", [P, P])
        rows = sb("rows", [P, 6, D])
        b0b, b1b, bmb, wjb, wib, we1b = (rows[:, c, :] for c in range(6))
        cols = sb("cols", [P, 16])
        we2, bi, bn = (cols[:, c:c + 1] for c in range(3))
        w3b, w4b, u3b, w5b, u5b = (cols[:, c:c + 1] for c in range(3, 8))
        wr, gb, be = (cols[:, c:c + 1] for c in range(8, 11))
        zb, rb, vb = (cols[:, c:c + 1] for c in range(11, 14))
        mhalf = sb("mhalf", [P, T])

        def small(tag):
            return (sb("st" + tag, [P, T, 6]), sb("mv" + tag, [P, T, 2]), sb("ve" + tag, [P, T]),
                    sb("rs" + tag, [P, T]))

        def layer_sets(tag, bank, idle, **b):
            f = dict(b, bank=bank, norm=small(tag))
            f["sv"] = sb("sv" + tag, [P, T, 3])
            f["sc"] = sb("sc" + tag, [P, 2])
            f["asrc"] = sb("asrc" + tag, [P, T])
            f["kb"] = idle[:, 0:D]
            f["bc"] = idle[:, D:3 * D].rearrange("p (i n) -> p i n", i=2)
            for name, per in (("xh", 2), ("xl", 2), ("xb", 2), ("m", 4), ("mc", 4), ("y", 6), ("sum", 6),
                              ("st", 3), ("p1", 9), ("p2", 6), ("mv", 3), ("ve", 3), ("rs", 3), ("xn", 3),
                              ("sj", 1), ("s", 1), ("sc", 1), ("k", 1), ("bc", 2), ("rw", 1), ("rx", 1),
                              ("kb", 1), ("kbx", 1), ("t", 4), ("tc", 4), ("g", 4), ("ex", 4), ("em", 4),
                              ("el", 4), ("as", 1), ("asb", 1), ("at", 2), ("atc", 2), ("e", T), ("ma", T),
                              ("ag", T), ("agc", 2), ("rsum", T - 1), ("rb", 2), ("self", 2)):
                f["s_" + name] = (sem(f"f{tag}_{name}"), per)
            return f

        main = layer_sets("m", FB, ring[1], xh=fxh, xl=fxl, m=fm, h=fh, z=fz, r=fr, v=fv)
        alt = layer_sets("a", GB, ring[2], xh=xh[1], xl=xl[1], m=z[0], h=hT[1], z=z[1], r=r, v=v)

        s_w, s_adj = sem("weights_loaded"), [sem(f"adj_loaded{t}") for t in range(T)]
        s_const, s_comb0, s_comb = sem("consts_set"), sem("weight_sums"), sem("weights_combined")
        s_wh, s_wl = sem("weight_hi"), sem("weight_lo")
        s_ah, s_al = sem("adj_hi_done"), sem("adj_lo_done")
        s_noedge, s_mask, s_mstore = sem("no_edge_done"), sem("mask_done"), sem("mask_stored")
        s_x = sems("x_loaded")
        s_mk = sems("mask_loaded")
        n_xh, n_xl, n_x, n_t, n_hc = sems("n_xh"), sems("n_xl"), sems("n_x"), sems("n_t"), sems("n_hc")
        n_th, n_tl = sems("n_th"), sems("n_tl")
        m_done, mh_done = sem("m_done"), sem("mh_done")
        z_pre, z_done, r_pre = sem("z_pre"), sem("z_done"), sem("r_pre")
        rh_done, rhh_done = sem("rh_done"), sem("rhh_done")
        v_pre, d_sub, d_mul = sem("v_pre"), sem("d_sub"), sem("d_mul")
        ml_done, r_done, rhl_done = sem("ml_done"), sem("r_done"), sem("rhl_done")
        v_done, h_new = sem("v_done"), sem("h_new")
        t_done, xh_done, xl_done = sem("t_done"), sem("xh_done"), sem("xl_done")
        th_done, tl_done = sems("th_done"), sems("tl_done")
        onorm = small("o")
        o_sems = {n: (sem("o_" + n), per) for n, per in (("st", 1), ("p1", 3), ("p2", 2), ("mv", 1), ("ve", 1),
                                                         ("rs", 1), ("xn", 1))}
        s_out = sems("z_moved")

        zflat = [z[s][:, :].rearrange("p (k d) -> p k d", d=D) for s in range(2)]
        rflat = r[:, :].rearrange("p (k d) -> p k d", d=D)
        stage = [fh, fz, fr, fv, ring[0], ring[1], ring[2], mk[0]]

        def cut(h):
            return slice(h * HALF, (h + 1) * HALF)

        def tile(t):
            return slice(t * P, (t + 1) * P)

        def nat(buf, h):
            return buf[:, h * HT:(h + 1) * HT, :]

        def bank4(b):
            return ps[:, b, :].rearrange("p (t d) -> p t d", d=D)

        def is_last(i):
            return isinstance(i, int) and i == STEPS - 1

        def turn(f, p, c, s):
            return dict(f, p=p, c=c, slot=s)

        def seen(eng, f, name, n, back=0):
            s, per = f["s_" + name]
            eng.wait_ge(s, f["p"] * (2 * per) + ((f["c"] - back) * per + n))

        def tell(ins, f, name):
            ins.then_inc(f["s_" + name][0], 1)

        def k4(p, i, s, h):
            return p * (4 * STEPS) + i * 4 + (2 * s + h + 1)

        FIRST = []
        attention = [n for names in BATCH for n in names.split() if n[0] in "se" and n != "sums"]
        for names in BATCH:
            for s in range(2):
                FIRST += [(n, s) for n in names.split() if n not in attention]
            if "s0" in names:
                FIRST += [(n, s) for s in range(2) for n in attention]
        SCHEDULE = [[(n, s) for n in names.split()] for s in range(2) for names in BATCH]

        def filler(piece, p):
            todo = list(SCHEDULE)

            def fill():
                if todo:
                    for name, s in todo.pop(0):
                        piece(name, turn(main, p, 1 + s, s))
            return fill, todo

        block = ctx.enter_context(nc.Block())

        @block.sync
        def _(sp):
            sp.dma_start(xf[0][:, :, :], x_in[0].rearrange("(t p) d -> p t d", p=P)).then_inc(s_x[0], 16)
            for t in range(0, T, 2):
                sp.dma_start(stage[t][:, :], adjT[tile(t), :]).then_inc(s_adj[t], 16)
            sp.dma_start(xf[1][:, :, :], x_in[1].rearrange("(t p) d -> p t d", p=P)).then_inc(s_x[1], 16)
            for s, names in enumerate((RAW0, RAW1)):
                for k, name in enumerate(names):
                    sp.dma_start(zflat[s][:, k, :], w[name]).then_inc(
                        s_w if k < len(names) - 1 else s_out[s], 16)

            def mask_tiles(f, first):
                for t in range(T):
                    if t >= 2:
                        seen(sp, f, "ma", t - 1)
                    elif not first:
                        seen(sp, f, "ma", T - 1 + t, back=1)
                    sp.dma_start(mk[t % 2][:, :], mask_dram[tile(t), :]).then_inc(s_mk[t % 2], 16)

            for t in range(T):
                sp.wait_ge(s_mask, t + 1)
                sp.dma_start(mask_dram[tile(t), :], stage[t][:, :]).then_inc(s_mstore, 16)
            sp.wait_ge(s_mstore, 16 * T)
            mask_tiles(turn(main, 0, 0, 0), True)
            for t in range(T):
                if t >= 2:
                    seen(sp, turn(alt, 0, 0, 1), "ma", t - 1)
                else:
                    seen(sp, turn(main, 0, 0, 0), "ma", T - 1 + t)
                sp.dma_start(mk[t % 2][:, :], mask_dram[tile(t), :]).then_inc(s_mk[t % 2], 16)

            def load(s, b, n):
                sp.wait_ge(n_tl[s], n)
                sp.dma_start(xf[s][:, :, :], x_in[b].rearrange("(t p) d -> p t d", p=P)).then_inc(s_x[s], 16)

            def pair(p, more):
                batch = p * 2 if isinstance(p, int) else sp.snap(p * 2)
                load(1, batch + 3, p + 1)
                mask_tiles(turn(main, p, 1, 0), False)
                mask_tiles(turn(main, p, 2, 1), False)
                if more:
                    load(0, batch + 4, p + 2)
                for s in range(2):
                    sp.wait_ge(o_sems["xn"][0], p * 2 + s + 1)
                    sp.dma_start(out[batch + s].rearrange("(t p) d -> p t d", p=P), zflat[s]
                                 ).then_inc(s_out[s], 16)

            load(0, 2, 1)
            with sp.Fori(0, LAST - 1) as p:
                pair(p, True)
            pair(LAST - 1, False)
            for s in range(2):
                sp.wait_ge(o_sems["xn"][0], LAST * 2 + s + 1)
                sp.dma_start(out[B - 2 + s].rearrange("(t p) d -> p t d", p=P), zflat[s]
                             ).then_inc(s_out[s], 16)
            for s in range(2):
                sp.wait_ge(s_out[s], 16 * (PAIRS + 1))

        NCOL = 11
        W_LOADS = len(RAW0) + len(RAW1) - 2 + NCOL + 6

        @block.gpsimd
        def _(pool):
            pool.memset(ones[:, :], 1.0).then_inc(s_const, 1)
            pool.memset(ident[:, :], 0.0).then_inc(s_const, 1)
            pool.memset(mhalf[:, :], -0.5).then_inc(s_const, 1)
            for f in (main, alt):
                pool.memset(f["sv"][:, :, 0:1], 1.0).then_inc(s_const, 1)
            pool.wait_ge(s_const, 5)
            pool.affine_select(out=ident[:, :], in_=ident[:, :], compare_op=ALU.not_equal, fill=1.0,
                               base=0, pattern=[[-1, P]], channel_multiplier=1).then_inc(s_const, 1)
            pool.wait_ge(s_w, 16 * W_LOADS)

            def add_bias(f, b):
                xs = xf[f["slot"]]
                tell(pool.tensor_tensor(xs[:, :, :], xs[:, :, :], b.unsqueeze(1).to_broadcast([P, T, D]), ALU.add),
                     f, "xb")

            def rstd(f, n):
                seen(pool, f, "ve", n + 1)
                tell(pool.tensor_tensor(f["norm"][3][:, :], f["norm"][2][:, :], mhalf[:, :], ALU.pow), f, "rs")

            def piece(name, f):
                if name == "x0":
                    seen(pool, f, "xl", 1)
                    add_bias(f, b0b)
                elif name in ("n0", "n1", "n2"):
                    rstd(f, int(name[1]))
                elif name == "proj":
                    seen(pool, f, "tc", 2)
                    add_bias(f, bmb)
                elif name[0] == "s" and name != "sums":
                    t = int(name[1])
                    if t == 0:
                        seen(pool, f, "el", 2)
                        return
                    if t > 1:
                        seen(pool, f, "rsum", t - 1)
                    seen(pool, f, "ma", t + 1)
                    tell(pool.tensor_tensor(f["r"][:, :], (ring[0] if t == 1 else f["r"])[:, :],
                                            ring[t % 3][:, :], ALU.add), f, "rsum")

            for name, s in FIRST:
                piece(name, turn((main, alt)[s], 0, 0, s))
            with pool.Fori(0, LAST) as p:
                fill, todo = filler(piece, p)
                while todo:
                    fill()
                for s in range(2):
                    pool.wait_ge(o_sems["ve"][0], p * 2 + s + 1)
                    pool.tensor_tensor(onorm[3][:, :], onorm[2][:, :], mhalf[:, :], ALU.pow).then_inc(o_sems["rs"][0], 1)
            for s in range(2):
                pool.wait_ge(o_sems["ve"][0], LAST * 2 + s + 1)
                pool.tensor_tensor(onorm[3][:, :], onorm[2][:, :], mhalf[:, :], ALU.pow).then_inc(o_sems["rs"][0], 1)

        @block.tensor
        def _(pe):
            def adj_product(dst, hi, lo, h, each_tile=False, halfway=lambda: None):
                for t in range(T):
                    if t == HT:
                        halfway()
                    if each_tile:
                        pe.wait_ge(s_al, t + 1)
                    for i, (a, b) in enumerate(((hi, adj_hi), (hi, adj_lo), (lo, adj_hi))):
                        mm = pe.matmul(dst, a[:, t, :], b[:, t, cut(h)],
                                       start=(t == 0 and i == 0), stop=(t == T - 1 and i == 2))
                return mm

            def passes(dst, k, hi, lo, first, last):
                pe.matmul(dst, wh[:, k, :], hi, start=first, stop=False, skip_group_check=True)
                pe.matmul(dst, wl[:, k, :], hi, start=False, stop=False, skip_group_check=True)
                return pe.matmul(dst, wh[:, k, :], lo, start=False, stop=last, skip_group_check=True)

            def turn_half(bank, src, h):
                for j in range(HT):
                    mm = pe.transpose(ps[:, bank, tile(j)], src(h * HT + j), ident[:, :])
                return mm

            def to_natural(f, h, parts):
                for j in range(HT):
                    t = h * HT + j
                    for i, (src, k) in enumerate(parts):
                        mm = pe.matmul(ps[:, f["bank"] + h, tile(j)], src[:, tile(t)], wf[:, k, :], start=(i == 0),
                                       stop=(i == len(parts) - 1), skip_group_check=True)
                tell(mm, f, "y")

            def piece(name, f):
                bank, xs = f["bank"], xf[f["slot"]]
                if name in ("m0a", "m0b", "m1a", "m1b"):
                    n, h = int(name[1]), "ab".index(name[2])
                    if h == 0:
                        seen(pe, f, "xl", n + 1)
                    if n == 1:
                        seen(pe, f, "sum", h + 1)
                    elif f["c"]:
                        seen(pe, f, "sum", 4 + h + 1, back=1)
                    tell(adj_product(ps[:, bank + h, :], f["xh"], f["xl"], h, f["c"] == 0 and n == 0), f, "m")
                elif name == "sums":
                    seen(pe, f, "sj", 1)
                    seen(pe, f, "mc", 3)
                    for t in range(T):
                        mm = pe.matmul(ps[:, bank, 0:2], xs[:, t, :], f["sv"][:, t, 0:2],
                                       start=(t == 0), stop=(t == T - 1))
                    tell(mm, f, "s")
                elif name == "rows":
                    seen(pe, f, "mc", 4)
                    seen(pe, f, "bc", 2)
                    for i in range(2):
                        mm = pe.matmul(ps[:, bank + 1, tile(i)], f["bc"][:, i, :], w1f[:, :], start=True, stop=True)
                    tell(mm, f, "rw")
                elif name in ("y0", "y1"):
                    n = int(name[1])
                    for h in range(2):
                        seen(pe, f, "mc", 2 * n + h + 1)
                        if n == 1:
                            seen(pe, f, "kb", 1)
                        to_natural(f, h, [(f["m"], (W0, W1R)[n])])
                elif name == "turn2":
                    seen(pe, f, "xn", 2)
                    for h in range(2):
                        tell(turn_half(bank + h, lambda t: xs[:, t, :], h), f, "t")
                elif name == "proj":
                    for h in range(2):
                        seen(pe, f, "tc", h + 1)
                        tell(pe.matmul(ps[:, bank + h, :], wf[:, WI, :], f["h"][:, cut(h)], start=True, stop=True),
                             f, "g")
                elif name == "turnh":
                    for h in range(2):
                        seen(pe, f, "el", h + 1)
                        tell(turn_half(bank + h, lambda t: f["m"][:, tile(t)], h), f, "t")
                elif name == "target":
                    for h in range(2):
                        seen(pe, f, "tc", 2 + h + 1)
                        tell(pe.matmul(ps[:, bank + h, :], we2b[:, :], f["m"][:, cut(h)], start=True, stop=True),
                             f, "at")
                elif name[0] == "e":
                    t = int(name[1])
                    if t == 0:
                        seen(pe, f, "atc", 2)
                    seen(pe, f, "ma", t + 1)
                    for h in range(2):
                        mm = pe.matmul(ps[:, bank + h, :], f["z"][:, tile(t)], ring[t % 3][:, cut(h)],
                                       start=(t == 0), stop=(t == T - 1))
                    tell(mm, f, "ag")
                elif name == "rowsum":
                    seen(pe, f, "rsum", T - 1)
                    for h in range(2):
                        seen(pe, f, "agc", h + 1)
                        tell(pe.matmul(ps[:, bank + h, :], ones[:, :], f["r"][:, cut(h)], start=True, stop=True),
                             f, "rb")
                elif name == "recv":
                    for h in range(2):
                        seen(pe, f, "self", h + 1)
                        pe.matmul(ps[:, bank + h, :], wf[:, WNA, :], f["h"][:, cut(h)], start=True, stop=False)
                        tell(pe.matmul(ps[:, bank + h, :], wf[:, WNB, :], f["v"][:, cut(h)], start=False, stop=True),
                             f, "g")
                elif name == "y2":
                    for h in range(2):
                        seen(pe, f, "el", 2 + h + 1)
                        to_natural(f, h, [(f["h"], WMA), (f["m"], WMB)])

            def start_slot(s, p):
                pe.wait_ge(n_xl[s], p + 1)
                if s == 0 and not isinstance(p, int):
                    pe.wait_ge(xl_done, k4(p, -1, 0, 1))
                for h in range(2):
                    if h:
                        pe.wait_ge(n_hc[s], p * 2 + 1)
                    turn_half(TB, lambda t: xf[s][:, t, :], h).then_inc(n_t[s], 1)

            def state_product(s, h, p, i, first, fill=lambda: None):
                if first:
                    pe.wait_ge(n_xl[s], p + 1)
                else:
                    pe.wait_ge(xl_done, k4(p, i - 1, s, 1))
                if s == 0 and h == 0:
                    if not first:
                        pe.wait_ge(ml_done, k4(p, i - 1, 1, 1))
                elif h == 1:
                    pe.wait_ge(ml_done, k4(p, i, s, 0))
                else:
                    pe.wait_ge(ml_done, k4(p, i, 0, 1))
                adj_product(ps[:, MB, :], xh[s], xl[s], h, halfway=fill).then_inc(m_done, 1)

            def candidate(s, p, i):
                for h in range(2):
                    pe.wait_ge(rhl_done, k4(p, i, s, h))
                    passes(ps[:, VB + h, :], U5, th[s][:, cut(h)], tl[s][:, cut(h)], False, True
                           ).then_inc(v_pre, 1)

            def turn_state(s, h, p, i):
                pe.wait_ge(h_new, k4(p, i, s, h))
                if h:
                    pe.wait_ge(xl_done, k4(p, i, s, 0))
                turn_half(TB, lambda t: hT[s][:, tile(t)], h).then_inc(t_done, 1)

            def gates(s, p, i, first, between):
                if first:
                    pe.wait_ge(n_tl[s], p + 1)
                else:
                    pe.wait_ge(tl_done[s], p * (STEPS - 1) + i)
                for h in range(2):
                    if s == 1:
                        pe.wait_ge(r_done, k4(p, i, 0, h))
                    elif not first:
                        pe.wait_ge(r_done, k4(p, i - 1, 1, h))
                    passes(ps[:, GB + h, :], U3, th[s][:, cut(h)], tl[s][:, cut(h)], True, False)
                between()
                for h in range(2):
                    pe.wait_ge(ml_done, k4(p, i, s, h))
                    passes(ps[:, GB + h, :], W3, mh[:, cut(h)], ml[:, cut(h)], False, True).then_inc(z_pre, 1)
                for h in range(2):
                    if s == 1:
                        pe.wait_ge(v_done, k4(p, i, 0, h))
                    elif not first:
                        pe.wait_ge(v_done, k4(p, i - 1, 1, h))
                    passes(ps[:, VB + h, :], W5, mh[:, cut(h)], ml[:, cut(h)], True, False)
                for h in range(2):
                    pe.wait_ge(z_done, k4(p, i, s, h))
                    passes(ps[:, GB + h, :], WD, mh[:, cut(h)], ml[:, cut(h)], False, True).then_inc(r_pre, 1)

            def steps(p, i, first, fill):
                if not first:
                    state_product(0, 0, p, i, first, fill)
                    fill()
                    candidate(1, p, i - 1)
                    fill()
                state_product(0, 1, p, i, first, fill)
                fill()
                if first:
                    start_slot(1, p)
                    gates(0, p, i, first, fill)
                else:
                    turn_state(1, 0, p, i - 1)
                    fill()
                    gates(0, p, i, first, lambda: (turn_state(1, 1, p, i - 1), fill()))
                fill()
                state_product(1, 0, p, i, first, fill)
                fill()
                candidate(0, p, i)
                fill()
                state_product(1, 1, p, i, first, fill)
                fill()
                turn_state(0, 0, p, i)
                fill()
                gates(1, p, i, first, lambda: (turn_state(0, 1, p, i), fill()))
                fill()

            for n, (name, s) in enumerate(FIRST):
                if name == "y0" and s == 0:
                    pe.wait_ge(s_const, 6)
                    pe.wait_ge(s_wl, 1)
                piece(name, turn((main, alt)[s], 0, 0, s))
            start_slot(0, 0)
            state_product(0, 0, 0, 0, True)
            with pe.Fori(0, LAST) as p:
                fill, todo = filler(piece, p)

                for i in range(STEPS):
                    steps(p, i, i == 0, fill)
                while todo:
                    fill()
                start_slot(0, p + 1)
                pe.wait_ge(ml_done, k4(p, STEPS - 1, 1, 1))
                state_product(0, 0, p + 1, 0, True)
                candidate(1, p, STEPS - 1)
                for h in range(2):
                    turn_state(1, h, p, STEPS - 1)
            steps(LAST, 0, True, lambda: None)
            with pe.Fori(1, STEPS - 1) as i:
                steps(LAST, i, False, lambda: None)
            steps(LAST, STEPS - 1, False, lambda: None)
            candidate(1, LAST, STEPS - 1)
            for h in range(2):
                turn_state(1, h, LAST, STEPS - 1)

        @block.scalar
        def _(act):
            for t in range(1, T, 2):
                act.dma_start(stage[t][:, :], adjT[tile(t), :]).then_inc(s_adj[t], 16)
            for c, name in enumerate(("we2", "bi", "bn", "w3_b", "w4_b", "u3_b", "w5_b", "u5_b")):
                act.dma_start(cols[:, c:c + 1], w[name]).then_inc(s_w, 16)
            for c, name in enumerate(("wr", "gb", "be")):
                act.dma_start(cols[:, 8 + c:9 + c], w[name].to_broadcast([P, 1])).then_inc(s_w, 16)
            for c, name in enumerate(("b0", "b1", "bm", "wj", "wi", "we1")):
                act.dma_start(rows[:, c, :], w[name].to_broadcast([P, D])).then_inc(s_w, 16)

            def copy(dst, src):
                return act.activation(dst, src, ACT.Copy)

            def piece(name, f):
                bank, xs = f["bank"], xf[f["slot"]]
                if name == "x0":
                    act.wait_ge(s_x[f["slot"]], f["p"] * 16 + (32 if f["c"] else 16))
                    tell(copy(f["xh"][:, :, :], xs[:, :, :]), f, "xh")
                if name in ("m0a", "m0b", "m1a", "m1b"):
                    n, h = int(name[1]), "ab".index(name[2])
                    seen(act, f, "m", 2 * n + h + 1)
                    tell(copy(f["m"][:, cut(h)], ps[:, bank + h, :]), f, "mc")
                elif name == "n0":
                    seen(act, f, "xn", 1)
                    tell(copy(f["xh"][:, :, :], xs[:, :, :]), f, "xh")
                elif name in ("turn2", "turnh"):
                    n = 0 if name == "turn2" else 2
                    for h in range(2):
                        seen(act, f, "t", n + h + 1)
                        tell(copy((f["h"] if n == 0 else f["z"])[:, cut(h)], ps[:, bank + h, :]), f, "tc")
                elif name in ("proj", "recv"):
                    n, b = (0, bi) if name == "proj" else (2, bn)
                    for h in range(2):
                        seen(act, f, "g", n + h + 1)
                        tell(act.activation(f["r"][:, cut(h)], ps[:, bank + h, :], ACT.Exp, bias=b), f, "ex")
                elif name == "target":
                    for h in range(2):
                        seen(act, f, "at", h + 1)
                        tell(copy(f["h"][:, cut(h)], ps[:, bank + h, :]), f, "atc")
                elif name[0] == "s" and name != "sums":
                    t = int(name[1])
                    if t == 0:
                        seen(act, f, "atc", 2)
                        seen(act, f, "asb", 1)
                        if f["s_e"] is alt["s_e"]:
                            seen(act, turn(main, 0, 0, 0), "ag", T)
                            seen(act, turn(main, 0, 0, 0), "rsum", T - 1)
                    if t >= 3:
                        seen(act, f, "ag", t - 2)
                        seen(act, f, "rsum", max(t - 3, 1))
                    tell(act.activation(ring[t % 3][:, :], f["h"][:, :], ACT.Sigmoid,
                                        bias=f["asrc"][:, t:t + 1]), f, "e")
                elif name == "e7":
                    seen(act, f, "ag", T)
                    for h in range(2):
                        tell(copy(f["h"][:, cut(h)], ps[:, bank + h, :]), f, "agc")

            def start_natural(s, p, fronts):
                act.wait_ge(main["s_xn"][0], fronts * 3)
                if s == 1:
                    act.wait_ge(alt["s_xn"][0], 3)
                copy(xh[s][:, :, :], xf[s][:, :, :]).then_inc(n_xh[s], 1)

            def start_turned(s, p):
                for h in range(2):
                    act.wait_ge(n_t[s], p * 2 + h + 1)
                    copy(hT[s][:, cut(h)], ps[:, TB, :]).then_inc(n_hc[s], 1)
                act.wait_ge(n_hc[s], p * 2 + 2)
                copy(th[s][:, :], hT[s][:, :]).then_inc(n_th[s], 1)

            def m_split(s, h, p, i):
                act.wait_ge(m_done, k4(p, i, s, h))
                copy(mh[:, cut(h)], ps[:, MB, :]).then_inc(mh_done, 1)

            def reset_hi(s, p, i):
                for h in range(2):
                    act.wait_ge(rh_done, k4(p, i, s, h))
                    copy(th[s][:, cut(h)], r[:, cut(h)]).then_inc(rhh_done, 1)

            def candidate(s, p, i, first=False):
                for h in range(2):
                    act.wait_ge(v_pre, k4(p, i, s, h))
                    if s == 1:
                        act.wait_ge(h_new, k4(p, i, 0, h))
                    elif not first:
                        act.wait_ge(h_new, k4(p, i - 1, 1, h))
                    act.activation(v[:, cut(h)], ps[:, VB + h, :], ACT.Tanh, bias=vb).then_inc(v_done, 1)

            def state_hi(s, h, p, i):
                if not is_last(i):
                    act.wait_ge(t_done, k4(p, i, s, h))
                    copy(nat(xh[s], h), bank4(TB)).then_inc(xh_done, 1)

            def gates(s, p, i, first):
                if first:
                    act.wait_ge(s_out[s], p * 16 + 16)
                for h in range(2):
                    act.wait_ge(z_pre, k4(p, i, s, h))
                    act.activation(z[s][:, cut(h)], ps[:, GB + h, :], ACT.Sigmoid, bias=zb).then_inc(z_done, 1)
                for h in range(2):
                    act.wait_ge(r_pre, k4(p, i, s, h))
                    if s == 1:
                        act.wait_ge(rhl_done, k4(p, i, 0, h))
                    elif not first:
                        act.wait_ge(rhl_done, k4(p, i - 1, 1, h))
                    act.activation(r[:, cut(h)], ps[:, GB + h, :], ACT.Sigmoid, bias=rb).then_inc(r_done, 1)

            def turned_hi(s, p, i):
                act.wait_ge(h_new, k4(p, i, s, 1))
                copy(th[s][:, :], hT[s][:, :]).then_inc(th_done[s], 1)

            def steps(p, i, fill):
                first = isinstance(i, int) and i == 0
                if not first:
                    reset_hi(1, p, i - 1)
                    fill()
                    fill()
                    m_split(0, 0, p, i)
                    fill()
                    candidate(1, p, i - 1)
                    fill()
                else:
                    start_natural(1, p, p * 2 + 1)
                fill()
                m_split(0, 1, p, i)
                fill()
                if first:
                    start_turned(1, p)
                else:
                    state_hi(1, 0, p, i - 1)
                    fill()
                    state_hi(1, 1, p, i - 1)
                fill()
                gates(0, p, i, first)
                if not first:
                    turned_hi(1, p, i - 1)
                reset_hi(0, p, i)
                fill()
                fill()
                m_split(1, 0, p, i)
                fill()
                candidate(0, p, i, first)
                fill()
                fill()
                m_split(1, 1, p, i)
                fill()
                state_hi(0, 0, p, i)
                fill()
                state_hi(0, 1, p, i)
                fill()
                gates(1, p, i, first)
                if not is_last(i):
                    turned_hi(0, p, i)

            begin = [(name, turn((main, alt)[s], 0, 0, s)) for name, s in FIRST]
            piece(*begin[0])
            for t in range(T):
                act.wait_ge(s_adj[t], 16)
                copy(adj_hi[:, t, :], stage[t][:, :]).then_inc(s_ah, 1)
            piece(*begin[1])
            act.wait_ge(s_comb, 1)
            copy(wh[:, :, :], rflat[:, 0:5, :]).then_inc(s_wh, 1)
            for args in begin[2:]:
                piece(*args)
            start_natural(0, 0, 1)
            start_turned(0, 0)
            m_split(0, 0, 0, 0)
            with act.Fori(0, LAST) as p:
                fill, todo = filler(piece, p)
                for i in range(STEPS):
                    steps(p, i, fill)
                reset_hi(1, p, STEPS - 1)
                while todo:
                    fill()
                start_natural(0, p + 1, p * 2 + 2)
                start_turned(0, p + 1)
                m_split(0, 0, p + 1, 0)
                candidate(1, p, STEPS - 1)
            steps(LAST, 0, lambda: None)
            with act.Fori(1, STEPS - 1) as i:
                steps(LAST, i, lambda: None)
            steps(LAST, STEPS - 1, lambda: None)
            reset_hi(1, LAST, STEPS - 1)
            candidate(1, LAST, STEPS - 1)

        @block.vector
        def _(dve):
            def lo(dst, src, hi):
                return dve.tensor_tensor(dst, src, hi.bitcast(F32), ALU.subtract)

            def norm_stats(src, bufs_, wait, sig):
                st, mv, ve, _ = bufs_
                for t in range(T):
                    ins = dve.bn_stats(st[:, t, :], src[:, t, :])
                sig(ins, "st")
                m_e, m_o, q_e, q_o = (st[:, :, c] for c in (1, 4, 2, 5))
                wait("st", 1)
                sig(dve.tensor_tensor(mv[:, :, 0], m_e, m_o, ALU.add), "p1")
                sig(dve.tensor_tensor(mv[:, :, 1], m_e, m_o, ALU.subtract), "p1")
                sig(dve.tensor_tensor(ve[:, :], q_e, q_o, ALU.add), "p1")
                wait("p1", 3)
                sig(dve.scalar_tensor_tensor(out=mv[:, :, 1], in0=mv[:, :, 1], scalar=0.25, in1=mv[:, :, 1],
                                             op0=ALU.mult, op1=ALU.mult), "p2")
                sig(dve.tensor_scalar(ve[:, :], ve[:, :], 1.0 / D, EPS, ALU.mult, ALU.add), "p2")
                sig(dve.tensor_scalar(mv[:, :, 0], mv[:, :, 0], 0.5, None, ALU.mult), "mv")
                wait("p2", 2)
                sig(dve.tensor_tensor(ve[:, :], ve[:, :], mv[:, :, 1], ALU.add), "ve")

            def norm_apply(src, bufs_, wait, sig):
                _, mv, _, rs = bufs_
                wait("mv", 1)
                wait("rs", 1)
                for t in range(T):
                    ins = dve.tensor_scalar(src[:, t, :], src[:, t, :], mv[:, t, 0:1], rs[:, t:t + 1],
                                            ALU.subtract, ALU.mult)
                sig(ins, "xn")

            def f_wait(f, n):
                def wait(name, c):
                    per = f["s_" + name][1] // 3
                    seen(dve, f, name, n * per + c)
                return wait

            def row_dots(junk, src, row, col):
                for t in range(T):
                    ins = dve.tensor_tensor_reduce(out=junk[:, tile(t)], in0=src[:, t, :], in1=row, scale=1.0,
                                                   scalar=0.0, op0=ALU.mult, op1=ALU.add, accum_out=col(t))
                return ins

            def elu(f, n, b, dst):
                for h in range(2):
                    seen(dve, f, "ex", n + h + 1)
                    tell(dve.tensor_scalar(f["r"][:, cut(h)], f["r"][:, cut(h)], 1.0, 1.0, ALU.min, ALU.subtract),
                         f, "em")
                    seen(dve, f, "em", n + h + 1)
                    tell(dve.scalar_tensor_tensor(out=dst[:, cut(h)], in0=ps[:, f["bank"] + h, :], scalar=b,
                                                  in1=f["r"][:, cut(h)], op0=ALU.add, op1=ALU.max), f, "el")

            def piece(name, f):
                bank, xs = f["bank"], xf[f["slot"]]
                if name == "x0":
                    seen(dve, f, "xh", 1)
                    tell(lo(f["xl"][:, :, :], xs[:, :, :], f["xh"][:, :, :]), f, "xl")
                elif name in ("y0", "y1", "y2"):
                    n = int(name[1])
                    if n == 0:
                        seen(dve, f, "xb", 1)
                    elif n == 1:
                        seen(dve, f, "kbx", 1)
                    else:
                        seen(dve, f, "xb", 2)
                    for h in range(2):
                        seen(dve, f, "y", 2 * n + h + 1)
                        tell(dve.tensor_tensor(nat(xs, h), bank4(bank + h), nat(xs, h), ALU.add), f, "sum")
                elif name in ("v0", "v1", "v2"):
                    n = int(name[1])
                    seen(dve, f, "sum", 2 * n + 2)
                    norm_stats(xs, f["norm"], f_wait(f, n), lambda ins, k: tell(ins, f, k))
                elif name in ("n0", "n1", "n2"):
                    n = int(name[1])
                    norm_apply(xs, f["norm"], f_wait(f, n), lambda ins, k: tell(ins, f, k))
                    if n == 0:
                        seen(dve, f, "xh", 2)
                        tell(lo(f["xl"][:, :, :], xs[:, :, :], f["xh"][:, :, :]), f, "xl")
                elif name == "m1a":
                    row_dots(f["v"], xs, wjb, lambda t: f["sv"][:, t, 1:2])
                    tell(row_dots(f["z"], xs, wib, lambda t: f["sv"][:, t, 2:3]), f, "sj")
                elif name == "sums":
                    seen(dve, f, "s", 1)
                    sc = f["sc"]
                    tell(dve.tensor_copy(sc[:, :], ps[:, bank, 0:2]), f, "sc")
                    seen(dve, f, "sc", 1)
                    tell(dve.scalar_tensor_tensor(out=sc[:, 1:2], in0=sc[:, 0:1], scalar=gb, in1=sc[:, 1:2],
                                                  op0=ALU.mult, op1=ALU.add), f, "k")
                    seen(dve, f, "k", 1)
                    for i in range(2):
                        tell(dve.tensor_scalar(f["bc"][:, i, :], ones[:, :], sc[:, i:i + 1], None, ALU.mult),
                             f, "bc")
                elif name == "rows":
                    seen(dve, f, "rw", 1)
                    for t in range(T):
                        ins = dve.scalar_tensor_tensor(out=xs[:, t, :], in0=ps[:, bank + 1, 0:P],
                                                       scalar=f["sv"][:, t, 2:3], in1=xs[:, t, :],
                                                       op0=ALU.mult, op1=ALU.add)
                    tell(ins, f, "rx")
                    tell(dve.tensor_tensor(f["kb"][:, :], ps[:, bank + 1, P:2 * P], b1b, ALU.add), f, "kb")
                    seen(dve, f, "rx", 1)
                    seen(dve, f, "kb", 1)
                    tell(dve.tensor_tensor(xs[:, :, :], xs[:, :, :],
                                           f["kb"][:, :].unsqueeze(1).to_broadcast([P, T, D]), ALU.add), f, "kbx")
                elif name == "proj":
                    elu(f, 0, bi, f["m"])
                elif name == "turnh":
                    seen(dve, f, "tc", 4)
                    tell(row_dots(f["v"], f["z"][:, :].rearrange("p (t d) -> p t d", d=D), we1b,
                                  lambda t: f["asrc"][:, t:t + 1]), f, "as")
                    seen(dve, f, "as", 1)
                    tell(dve.tensor_scalar(f["asrc"][:, :], f["asrc"][:, :], be, None, ALU.add), f, "asb")
                elif name == "recv":
                    elu(f, 2, bn, f["h"])
                elif name == "rowsum":
                    for h in range(2):
                        seen(dve, f, "rb", h + 1)
                        tell(dve.tensor_tensor(f["v"][:, cut(h)], ps[:, bank + h, :], f["m"][:, cut(h)], ALU.mult),
                             f, "self")
                elif name[0] == "s":
                    t = int(name[1])
                    if f["s_e"] is alt["s_e"]:
                        dve.wait_ge(s_mk[t % 2], 16 * (T // 2 + t // 2 + 1))
                    else:
                        before = (f["c"] + 1 if f["c"] else 0) * T // 2
                        dve.wait_ge(s_mk[t % 2], f["p"] * (16 * T) + 16 * (before + t // 2 + 1))
                    seen(dve, f, "e", t + 1)
                    tell(dve.tensor_tensor(ring[t % 3][:, :], ring[t % 3][:, :], mk[t % 2][:, :], ALU.mult),
                         f, "ma")

            def start_natural(s, p):
                dve.wait_ge(n_xh[s], p + 1)
                lo(xl[s][:, :, :], xf[s][:, :, :], xh[s][:, :, :]).then_inc(n_xl[s], 1)
                dve.tensor_copy(x[s][:, :, :], xf[s][:, :, :]).then_inc(n_x[s], 1)

            def start_turned(s, p):
                dve.wait_ge(n_th[s], p + 1)
                lo(tl[s][:, :], hT[s][:, :], th[s][:, :]).then_inc(n_tl[s], 1)

            def m_split(s, h, p, i):
                dve.wait_ge(mh_done, k4(p, i, s, h))
                lo(ml[:, cut(h)], ps[:, MB, :], mh[:, cut(h)]).then_inc(ml_done, 1)

            def reset(s, p, i):
                for h in range(2):
                    dve.wait_ge(r_done, k4(p, i, s, h))
                    dve.tensor_tensor(r[:, cut(h)], r[:, cut(h)], hT[s][:, cut(h)], ALU.mult).then_inc(rh_done, 1)

            def reset_lo(s, p, i):
                for h in range(2):
                    dve.wait_ge(rhh_done, k4(p, i, s, h))
                    lo(tl[s][:, cut(h)], r[:, cut(h)], th[s][:, cut(h)]).then_inc(rhl_done, 1)

            def update(s, p, i):
                for h in range(2):
                    dve.wait_ge(v_done, k4(p, i, s, h))
                    dve.tensor_tensor(v[:, cut(h)], v[:, cut(h)], hT[s][:, cut(h)], ALU.subtract).then_inc(d_sub, 1)
                    dve.wait_ge(d_sub, k4(p, i, s, h))
                    dve.tensor_tensor(v[:, cut(h)], v[:, cut(h)], z[s][:, cut(h)], ALU.mult).then_inc(d_mul, 1)
                    dve.wait_ge(d_mul, k4(p, i, s, h))
                    dve.tensor_tensor(hT[s][:, cut(h)], hT[s][:, cut(h)], v[:, cut(h)], ALU.add).then_inc(h_new, 1)

            def state_lo(s, h, p, i):
                if is_last(i):
                    dve.wait_ge(t_done, k4(p, i, s, h))
                    dve.tensor_tensor(nat(zflat[s], h), bank4(TB), nat(x[s], h), ALU.add).then_inc(xl_done, 1)
                else:
                    dve.wait_ge(xh_done, p * (4 * (STEPS - 1)) + i * 4 + (2 * s + h + 1))
                    lo(nat(xl[s], h), bank4(TB), nat(xh[s], h)).then_inc(xl_done, 1)

            def turned_lo(s, p, i):
                dve.wait_ge(th_done[s], p * (STEPS - 1) + i + 1)
                lo(tl[s][:, :], hT[s][:, :], th[s][:, :]).then_inc(tl_done[s], 1)

            def steps(p, i, fill):
                first = isinstance(i, int) and i == 0
                if not first:
                    reset(1, p, i - 1)
                    turned_lo(0, p, i - 1)
                    reset_lo(1, p, i - 1)
                    fill()
                    fill()
                    m_split(0, 0, p, i)
                    fill()
                    update(1, p, i - 1)
                    fill()
                else:
                    start_natural(1, p)
                fill()
                m_split(0, 1, p, i)
                fill()
                if first:
                    start_turned(1, p)
                else:
                    state_lo(1, 0, p, i - 1)
                    fill()
                    state_lo(1, 1, p, i - 1)
                fill()
                reset(0, p, i)
                if not first:
                    turned_lo(1, p, i - 1)
                reset_lo(0, p, i)
                fill()
                fill()
                m_split(1, 0, p, i)
                fill()
                update(0, p, i)
                fill()
                fill()
                m_split(1, 1, p, i)
                fill()
                state_lo(0, 0, p, i)
                fill()
                state_lo(0, 1, p, i)
                fill()

            def output(s, p):
                o_wait = lambda name, c: dve.wait_ge(o_sems[name][0], p * (2 * o_sems[name][1])
                                                     + (s * o_sems[name][1] + c))
                o_tell = lambda ins, name: ins.then_inc(o_sems[name][0], 1)

                def stats():
                    dve.wait_ge(xl_done, k4(p, STEPS - 1, s, 1))
                    norm_stats(zflat[s], onorm, o_wait, o_tell)
                return stats, lambda: norm_apply(zflat[s], onorm, o_wait, o_tell)

            begin = [(name, turn((main, alt)[s], 0, 0, s)) for name, s in FIRST]
            piece(*begin[0])
            for t in range(T):
                dve.wait_ge(s_ah, t + 1)
                lo(adj_lo[:, t, :], stage[t][:, :], adj_hi[:, t, :]).then_inc(s_al, 1)
            piece(*begin[1])
            dve.wait_ge(s_w, 16 * W_LOADS)
            for s in range(2):
                dve.wait_ge(s_out[s], 16)
            dve.tensor_copy(wf[:, :, :], zflat[0][:, 0:7, :]).then_inc(s_comb0, 1)
            dve.tensor_copy(w1f[:, :], zflat[0][:, 1, :]).then_inc(s_comb0, 1)
            dve.tensor_copy(rflat[:, U3, :], zflat[0][:, 7, :]).then_inc(s_comb0, 1)
            dve.tensor_tensor(rflat[:, W3, :], zflat[1][:, 0, :], zflat[1][:, 1, :], ALU.add).then_inc(s_comb0, 1)
            dve.tensor_tensor(rflat[:, 5, :], zflat[1][:, 2, :], zflat[1][:, 3, :], ALU.add).then_inc(s_comb0, 1)
            dve.tensor_tensor(rflat[:, W5, :], zflat[1][:, 4, :], zflat[1][:, 5, :], ALU.add).then_inc(s_comb0, 1)
            dve.tensor_copy(rflat[:, U5, :], zflat[1][:, 6, :]).then_inc(s_comb0, 1)
            dve.tensor_tensor(zb, w3b, u3b, ALU.add).then_inc(s_comb0, 1)
            dve.tensor_tensor(rb, w4b, u3b, ALU.add).then_inc(s_comb0, 1)
            dve.tensor_tensor(vb, w5b, u5b, ALU.add).then_inc(s_comb0, 1)
            dve.wait_ge(s_const, 6)
            dve.tensor_scalar(we2b[:, :], ones[:, :], we2, None, ALU.mult).then_inc(s_comb0, 1)
            dve.wait_ge(s_comb0, 11)
            dve.tensor_scalar(wf[:, W1R, :], w1f[:, :], wr, None, ALU.mult).then_inc(s_comb0, 1)
            dve.tensor_tensor(rflat[:, WD, :], rflat[:, 5, :], rflat[:, W3, :], ALU.subtract).then_inc(s_comb, 1)
            dve.wait_ge(s_wh, 1)
            dve.wait_ge(s_comb0, 12)
            lo(wl[:, :, :], rflat[:, 0:5, :], wh[:, :, :]).then_inc(s_wl, 1)
            for t in range(T):
                if t >= 1:
                    dve.wait_ge(s_mask, t)
                dve.wait_ge(s_al, t + 1)
                dve.tensor_scalar(mk[1][:, :], stage[t][:, :], 0.0, ALPHA, ALU.is_equal, ALU.mult
                                  ).then_inc(s_noedge, 1)
                dve.wait_ge(s_noedge, t + 1)
                dve.tensor_tensor(stage[t][:, :], stage[t][:, :], mk[1][:, :], ALU.add).then_inc(s_mask, 1)
            dve.wait_ge(s_mask, T)
            dve.wait_ge(s_mstore, 16 * T)
            for args in begin[2:]:
                piece(*args)
            start_natural(0, 0)
            start_turned(0, 0)
            m_split(0, 0, 0, 0)
            with dve.Fori(0, LAST) as p:
                fill, todo = filler(piece, p)
                for i in range(STEPS):
                    steps(p, i, fill)
                reset(1, p, STEPS - 1)
                reset_lo(1, p, STEPS - 1)
                while todo:
                    fill()
                start_natural(0, p + 1)
                stats, apply = output(0, p)
                stats()
                start_turned(0, p + 1)
                m_split(0, 0, p + 1, 0)
                update(1, p, STEPS - 1)
                apply()
                for h in range(2):
                    state_lo(1, h, p, STEPS - 1)
                for part in output(1, p):
                    part()
            steps(LAST, 0, lambda: None)
            with dve.Fori(1, STEPS - 1) as i:
                steps(LAST, i, lambda: None)
            steps(LAST, STEPS - 1, lambda: None)
            reset(1, LAST, STEPS - 1)
            reset_lo(1, LAST, STEPS - 1)
            stats, apply = output(0, LAST)
            stats()
            update(1, LAST, STEPS - 1)
            apply()
            for h in range(2):
                state_lo(1, h, LAST, STEPS - 1)
            for part in output(1, LAST):
                part()


def kernel(**inputs):
    import numpy as _np
    import concourse.bacc as _bacc
    from concourse import mybir as _mybir
    from concourse.bass_utils import run_bass_kernel_spmd as _run

    a = {k: _np.asarray(v) for k, v in inputs.items()}
    D = a["x"].shape[2]
    lay = {
        "x": a["x"], "adjT": a["adj"].T,
        "W0": a["L0_gnn_weight"], "b0": a["L0_gnn_bias"].reshape(1, D),
        "wj": a["L1_gnn_g_w"][:D].reshape(1, D), "wi": a["L1_gnn_g_w"][D:2 * D].reshape(1, D),
        "wr": a["L1_gnn_g_w"][2 * D:].reshape(1, 1), "gb": a["L1_gnn_g_b"].reshape(1, 1),
        "W1": a["L1_gnn_weight"], "b1": a["L1_gnn_bias"].reshape(1, D),
        "Wi": a["L2_gnn_Wi"], "bi": a["L2_gnn_bi"].reshape(D, 1),
        "we1": a["L2_gnn_We"][:D].reshape(1, D), "we2": a["L2_gnn_We"][D:], "be": a["L2_gnn_be"].reshape(1, 1),
        "WnA": a["L2_gnn_Wn"][:D], "WnB": a["L2_gnn_Wn"][D:], "bn": a["L2_gnn_bn"].reshape(D, 1),
        "WmA": a["L2_gnn_Wm"][:D], "WmB": a["L2_gnn_Wm"][D:], "bm": a["L2_gnn_bm"].reshape(1, D),
        "w3a": a["L3_gnn_w3_w"][:, :D].T, "w3b": a["L3_gnn_w3_w"][:, D:].T,
        "w4a": a["L3_gnn_w4_w"][:, :D].T, "w4b": a["L3_gnn_w4_w"][:, D:].T,
        "w5a": a["L3_gnn_w5_w"][:, :D].T, "w5b": a["L3_gnn_w5_w"][:, D:].T,
        "u3": a["L3_gnn_u3_w"].T, "u5": a["L3_gnn_u5_w"].T,
        "w3_b": a["L3_gnn_w3_b"].reshape(D, 1), "w4_b": a["L3_gnn_w4_b"].reshape(D, 1),
        "w5_b": a["L3_gnn_w5_b"].reshape(D, 1), "u3_b": a["L3_gnn_u3_b"].reshape(D, 1),
        "u5_b": a["L3_gnn_u5_b"].reshape(D, 1),
    }
    nc = _bacc.Bacc("TRN2", target_bir_lowering=False, num_devices=1)
    arrays, aps = {}, {}
    for name, v in lay.items():
        v = _np.ascontiguousarray(v)
        arrays[f"in_{name}"] = v
        aps[name] = nc.dram_tensor(f"in_{name}", v.shape, _mybir.dt.from_np(v.dtype), kind="ExternalInput").ap()
    out = nc.dram_tensor("out", a["x"].shape, _mybir.dt.from_np(a["x"].dtype), kind="ExternalOutput").ap()
    mask = nc.dram_tensor("mask_scratch", a["adj"].shape, _mybir.dt.float32, kind="Internal").ap()
    program(nc, aps["x"], aps["adjT"], aps, mask, out)
    res = _run(nc, [arrays], core_ids=[0])
    return res.results[0]["out"]
```

```python
from contextlib import ExitStack

import concourse.bass as bass
from concourse import mybir

P = 128
HALF = 512
ALPHA = 0.005
EPS = 1e-5
STEPS = 5

ALU = mybir.AluOpType
ACT = mybir.ActivationFunctionType
F32 = mybir.dt.float32
F32R = mybir.dt.float32r

(U3, W3, WD, W5, U5) = range(5)
(W0, W1R, WI, WNA, WNB, WMA, WMB) = range(7)
FB, MB, TB, GB, VB = 0, 2, 3, 4, 6
BATCHES = (["", "x0", "", "m0a m0b", "", "", "y0", "v0", "", "n0", "", "", "", "m1a", "", "m1b sums", "",
            "rows", "", "y1", "", "v1", "n1", "", "turn2", "proj", "", "", "turnh", "", "", "target s0", "s1",
            "", "", "e0 s2", "", "", "e1 s3 e2 s4 e3 s5 e4 s6", "e5", "", "s7 e6 e7", "", "rowsum", "", "recv",
            "", "y2", "v2", "", "", "n2"],
           ["x0", "", "", "m0a m0b", "", "y0", "v0", "", "n0", "", "", "", "m1a m1b sums", "rows", "", "",
            "y1 v1", "", "", "n1", "", "turn2", "proj", "", "", "", "turnh", "", "target s0", "", "",
            "s1 e0 s2", "", "", "", "e1", "s3 e2 s4 e3 s5 e4 s6 e5 s7", "e6 e7", "", "rowsum", "recv", "",
            "y2 v2", "n2"])
START = """x0:0 x0:1 m0a:0 m0b:0 y0:0 v0:0 weights:0 m0a:1 n0:0 m0b:1 y0:1 v0:1 m1a:0 n0:1 m1b:0 mask2:0 sums:0
           rows:0 m1a:1 mask3:0 y1:0 v1:0 mask4:0 n1:0 mask5:0 m1b:1 mask6:0 mask7:0 sums:1 turn2:0 proj:0
           rows:1 y1:1 v1:1 turnh:0 target:0 n1:1 s0:0 s1:0 s2:0 turn2:1 e0:0 s3:0 e1:0 proj:1 s4:0 e2:0 s5:0
           e3:0 s6:0 turnh:1 target:1 e4:0 s7:0 e5:0 e6:0 e7:0 s0:1 s1:1 rowsum:0 s2:1 e0:1 s3:1 recv:0 e1:1
           s4:1 e2:1 s5:1 y2:0 e3:1 v2:0 n2:0 s6:1 e4:1 s7:1 e5:1 e6:1 e7:1"""
TAIL = ["rowsum", "", "", "recv", "y2", "", "v2", "n2"]

BETWEEN = 9


def program(nc, x_in, adjT, w, mask_dram, out):
    B, N, D = x_in.shape
    T = N // P
    PAIRS = B // 2
    LAST = PAIRS - 1
    assert D == P and N == 2 * HALF and B % 2 == 0
    HT = T // 2

    with ExitStack() as ctx:
        def sb(name, shape, dt=F32):
            return ctx.enter_context(nc.sbuf_tensor(name, shape, dt))

        def sem(name):
            return ctx.enter_context(nc.semaphore(name))

        def sems(name):
            return [sem(f"{name}{s}") for s in range(2)]

        def bufs(name, shape, dt=F32):
            return [sb(f"{name}{s}", shape, dt) for s in range(2)]

        ps = ctx.enter_context(nc.psum_tensor("ps", [P, 8, HALF], F32))

        adj_hi = sb("adj_hi", [P, T, N], F32R)
        adj_lo = sb("adj_lo", [P, T, N], F32R)
        x = bufs("x", [P, T, D])
        xh = bufs("xh", [P, T, D], F32R)
        xl = bufs("xl", [P, T, D], F32R)
        hT = bufs("hT", [P, N])
        th = bufs("th", [P, N], F32R)
        tl = bufs("tl", [P, N], F32R)
        z = bufs("z", [P, N])
        mh = sb("mh", [P, N], F32R)
        ml = sb("ml", [P, N], F32R)
        r = sb("r", [P, N])
        v = sb("v", [P, N])
        xf = bufs("xf", [P, T, D])
        fxh = sb("fxh", [P, T, D], F32R)
        fxl = sb("fxl", [P, T, D], F32R)
        fm = sb("fm", [P, N])
        fh = sb("fh", [P, N])
        fz = sb("fz", [P, N])
        fr = sb("fr", [P, N])
        fv = sb("fv", [P, N])
        ring = [sb(f"ring{i}", [P, N]) for i in range(3)]
        mk = [sb(f"mk{i}", [P, N]) for i in range(2)]

        wh = sb("wh", [P, 5, D], F32R)
        wl = sb("wl", [P, 5, D], F32R)
        wf = sb("wf", [P, 7, D])
        w1f = sb("w1f", [P, D])
        we2b = sb("we2b", [P, D])
        ones = sb("ones", [P, P])
        ident = sb("ident", [P, P])
        rows = sb("rows", [P, 6, D])
        b0b, b1b, bmb, wjb, wib, we1b = (rows[:, c, :] for c in range(6))
        cols = sb("cols", [P, 16])
        we2, bi, bn = (cols[:, c:c + 1] for c in range(3))
        w3b, w4b, u3b, w5b, u5b = (cols[:, c:c + 1] for c in range(3, 8))
        wr, gb, be = (cols[:, c:c + 1] for c in range(8, 11))
        zb, rb, vb = (cols[:, c:c + 1] for c in range(11, 14))
        mhalf = sb("mhalf", [P, T])

        def small(tag):
            return (sb("st" + tag, [P, T, 6]), sb("mv" + tag, [P, T, 2]), sb("ve" + tag, [P, T]),
                    sb("rs" + tag, [P, T]))

        def layer_sets(tag, bank, idle, **b):
            f = dict(b, bank=bank, norm=small(tag))
            f["sv"] = sb("sv" + tag, [P, T, 3])
            f["sc"] = sb("sc" + tag, [P, 2])
            f["asrc"] = sb("asrc" + tag, [P, T])
            f["kb"] = idle[:, 0:D]
            f["bc"] = idle[:, D:3 * D].rearrange("p (i n) -> p i n", i=2)
            for name, per in (("xh", 2), ("xl", 2), ("xb", 2), ("m", 4), ("mc", 4), ("y", 6), ("sum", 6),
                              ("st", 3), ("p1", 9), ("p2", 6), ("mv", 3), ("ve", 3), ("rs", 3), ("xn", 3),
                              ("sj", 1), ("s", 1), ("sc", 1), ("k", 1), ("bc", 2), ("rw", 1), ("rx", 1),
                              ("kb", 1), ("kbx", 1), ("t", 4), ("tc", 4), ("g", 4), ("ex", 4), ("em", 4),
                              ("el", 4), ("as", 1), ("asb", 1), ("at", 2), ("atc", 2), ("e", T), ("ma", T),
                              ("ag", T), ("agc", 2), ("rsum", T - 1), ("rb", 2), ("self", 2)):
                f["s_" + name] = (sem(f"f{tag}_{name}"), per)
            return f

        main = layer_sets("m", FB, ring[1], xh=fxh, xl=fxl, m=fm, h=fh, z=fz, r=fr, v=fv)
        alt = layer_sets("a", GB, ring[2], xh=xh[1], xl=xl[1], m=z[0], h=hT[1], z=z[1], r=r, v=v)

        s_w0, s_w, s_wv = sem("W0_loaded"), sem("weights_loaded"), sem("vectors_loaded")
        s_adj = [sem(f"adj_loaded{t}") for t in range(T)]
        s_const, s_comb0, s_comb = sem("consts_set"), sem("weight_sums"), sem("weights_combined")
        s_wh, s_wl = sem("weight_hi"), sem("weight_lo")
        s_ah, s_al = sem("adj_hi_done"), sem("adj_lo_done")
        s_noedge, s_mask, s_mstore = sem("no_edge_done"), sem("mask_done"), sem("mask_stored")
        s_pnoedge, s_pmask = sem("pool_no_edge_done"), sem("pool_mask_done")
        s_x = sems("x_loaded")
        s_mk = sems("mask_loaded")
        n_xh, n_xl, n_x, n_t, n_hc = sems("n_xh"), sems("n_xl"), sems("n_x"), sems("n_t"), sems("n_hc")
        n_th, n_tl = sems("n_th"), sems("n_tl")
        m_done, mh_done = sem("m_done"), sem("mh_done")
        z_pre, z_done, r_pre = sem("z_pre"), sem("z_done"), sem("r_pre")
        rh_done, rhh_done = sem("rh_done"), sem("rhh_done")
        v_pre, d_sub, d_mul = sem("v_pre"), sem("d_sub"), sem("d_mul")
        ml_done, r_done, rhl_done = sem("ml_done"), sem("r_done"), sem("rhl_done")
        v_done, h_new = sem("v_done"), sem("h_new")
        t_done, xh_done, xl_done = sem("t_done"), sem("xh_done"), sem("xl_done")
        th_done, tl_done = sems("th_done"), sems("tl_done")
        onorm = small("o")
        o_sems = {n: (sem("o_" + n), per) for n, per in (("st", 1), ("p1", 3), ("p2", 2), ("mv", 1), ("ve", 1),
                                                         ("rs", 1), ("xn", 1))}
        s_out = sems("z_moved")

        zflat = [z[s][:, :].rearrange("p (k d) -> p k d", d=D) for s in range(2)]
        rflat = r[:, :].rearrange("p (k d) -> p k d", d=D)
        stage = ([x[s][:, :, :].rearrange("p t d -> p (t d)") for s in range(2)]
                 + [b[:, :] for b in (hT[0], mk[0], mk[1], ring[0], hT[1], fz)])
        noedge = z[1]
        POOLED = 2

        def cut(h):
            return slice(h * HALF, (h + 1) * HALF)

        def tile(t):
            return slice(t * P, (t + 1) * P)

        def nat(buf, h):
            return buf[:, h * HT:(h + 1) * HT, :]

        def bank4(b):
            return ps[:, b, :].rearrange("p (t d) -> p t d", d=D)

        def is_last(i):
            return isinstance(i, int) and i == STEPS - 1

        def is_first(i):
            return isinstance(i, int) and i == 0

        def turn(f, p, c, s):
            return dict(f, p=p, c=c, slot=s)

        def seen(eng, f, name, n, back=0):
            s, per = f["s_" + name]
            eng.wait_ge(s, f["p"] * (2 * per) + ((f["c"] - back) * per + n))

        def tell(ins, f, name):
            ins.then_inc(f["s_" + name][0], 1)

        def nth_half(p, i, s, h):
            return p * (4 * STEPS) + i * 4 + (2 * s + h + 1)

        FIRST = [(n.split(":")[0], int(n[-1])) for n in START.split()]
        SCHEDULE = [[(n, s) for n in names.split()] for s, batch in enumerate(BATCHES)
                    for names in batch]

        def filler(piece, p):
            todo = list([names.split() for names in TAIL] if p is None else SCHEDULE)

            def fill():
                if todo:
                    for names in todo.pop(0):
                        if p is None:
                            piece(names, turn(alt, 0, 0, 1))
                        else:
                            piece(names[0], turn(main, p, 1 + names[1], names[1]))
            return fill

        def units(p):
            order = [(s, p, i) for i in range(STEPS) for s in range(2)] + [(0, p + 1, 0)]
            return list(zip(order[1:], order))

        def last_pair(eng, unit, idle):
            unit((1, LAST, 0), (0, LAST, 0), idle)
            with eng.Fori(1, STEPS - 1) as i:
                unit((0, LAST, i), (1, LAST, i - 1), idle)
                unit((1, LAST, i), (0, LAST, i), idle)
            unit((0, LAST, STEPS - 1), (1, LAST, STEPS - 2), idle)
            unit((1, LAST, STEPS - 1), (0, LAST, STEPS - 1), idle)

        block = ctx.enter_context(nc.Block())

        @block.sync
        def _(sp):
            def first_state(s):
                sp.dma_start(xf[s][:, :, :], x_in[s].rearrange("(t p) d -> p t d", p=P)).then_inc(s_x[s], 16)

            first_state(0)
            for t in range(T):
                if t >= 2:
                    sp.wait_ge(s_adj[t - 2], 16)
                sp.dma_start(stage[t], adjT[tile(t), :]).then_inc(s_adj[t], 16)
                if t == HT:
                    first_state(1)
                elif t == HT + 1:
                    sp.dma_start(wf[:, W0, :], w["W0"]).then_inc(s_w0, 16)
            sp.dma_start(z[1][:, 0:6 * D], w["halves"]).then_inc(s_w, 16)
            sp.dma_start(wf[:, WI:WMB + 1, :].rearrange("p c d -> p (c d)"), w["W2"]).then_inc(s_w, 16)
            sp.dma_start(w1f[:, :], w["W1"]).then_inc(s_w, 16)
            sp.dma_start(rflat[:, U3, :], w["u3"]).then_inc(s_out[0], 16)
            sp.dma_start(rflat[:, U5, :], w["u5"]).then_inc(s_out[1], 16)

            def mask_tiles(f, first):
                for t in range(T):
                    if t >= 2:
                        seen(sp, f, "ma", t - 1)
                    elif not first:
                        seen(sp, f, "ma", T - 1 + t, back=1)
                    sp.dma_start(mk[t % 2][:, :], mask_dram[tile(t), :]).then_inc(s_mk[t % 2], 16)

            for t in range(T):
                if t < POOLED:
                    sp.wait_ge(s_pmask, t + 1)
                else:
                    sp.wait_ge(s_mask, t + 1 - POOLED)
                sp.dma_start(mask_dram[tile(t), :], stage[t]).then_inc(s_mstore, 16)
            sp.wait_ge(s_mstore, 16 * T)
            mask_tiles(turn(main, 0, 0, 0), True)
            for t in range(T):
                if t >= 2:
                    seen(sp, turn(alt, 0, 0, 1), "ma", t - 1)
                else:
                    seen(sp, turn(main, 0, 0, 0), "ma", T - 1 + t)
                sp.dma_start(mk[t % 2][:, :], mask_dram[tile(t), :]).then_inc(s_mk[t % 2], 16)

            def load(s, b, n):
                sp.wait_ge(n_tl[s], n)
                sp.dma_start(xf[s][:, :, :], x_in[b].rearrange("(t p) d -> p t d", p=P)).then_inc(s_x[s], 16)

            def pair(p, more):
                batch = p * 2 if isinstance(p, int) else sp.snap(p * 2)
                load(1, batch + 3, p + 1)
                mask_tiles(turn(main, p, 1, 0), False)
                mask_tiles(turn(main, p, 2, 1), False)
                for s in range(2):
                    sp.wait_ge(o_sems["xn"][0], p * 2 + s + 1)
                    sp.dma_start(out[batch + s].rearrange("(t p) d -> p t d", p=P), zflat[s]
                                 ).then_inc(s_out[s], 16)
                    if more and s == 0:
                        load(0, batch + 4, p + 2)

            load(0, 2, 1)
            with sp.Fori(0, LAST - 1) as p:
                pair(p, True)
            pair(LAST - 1, False)
            for s in range(2):
                sp.wait_ge(o_sems["xn"][0], LAST * 2 + s + 1)
                sp.dma_start(out[B - 2 + s].rearrange("(t p) d -> p t d", p=P), zflat[s]
                             ).then_inc(s_out[s], 16)
            for s in range(2):
                sp.wait_ge(s_out[s], 16 * (PAIRS + 1))

        W_LOADS, V_LOADS = 3, 3

        @block.gpsimd
        def _(pool):
            pool.dma_start(cols[:, 0:8], w["columns"]).then_inc(s_wv, 16)
            pool.dma_start(cols[:, 8:11], w["scalars"].to_broadcast([P, 3])).then_inc(s_wv, 16)
            pool.dma_start(rows[:, :, :].rearrange("p c d -> p (c d)"), w["rows"].to_broadcast([P, 6 * D])
                           ).then_inc(s_wv, 16)
            pool.memset(ones[:, :], 1.0).then_inc(s_const, 1)
            pool.memset(ident[:, :], 0.0).then_inc(s_const, 1)
            pool.memset(mhalf[:, :], -0.5).then_inc(s_const, 1)
            for f in (main, alt):
                pool.memset(f["sv"][:, :, 0:1], 1.0).then_inc(s_const, 1)
            pool.wait_ge(s_const, 5)
            pool.affine_select(out=ident[:, :], in_=ident[:, :], compare_op=ALU.not_equal, fill=1.0,
                               base=0, pattern=[[-1, P]], channel_multiplier=1).then_inc(s_const, 1)
            def pool_mask(t):
                if t:
                    pool.wait_ge(s_pmask, t)
                pool.wait_ge(s_al, t + 1)
                pool.tensor_scalar(ring[1][:, :], stage[t], 0.0, ALPHA, ALU.is_equal, ALU.mult).then_inc(s_pnoedge, 1)
                pool.wait_ge(s_pnoedge, t + 1)
                pool.tensor_tensor(stage[t], stage[t], ring[1][:, :], ALU.add).then_inc(s_pmask, 1)

            pool.wait_ge(s_wv, 16 * V_LOADS)

            def add_bias(f, b):
                xs = xf[f["slot"]]
                tell(pool.tensor_tensor(xs[:, :, :], xs[:, :, :], b.unsqueeze(1).to_broadcast([P, T, D]), ALU.add),
                     f, "xb")

            def rstd(f, n):
                seen(pool, f, "ve", n + 1)
                tell(pool.tensor_tensor(f["norm"][3][:, :], f["norm"][2][:, :], mhalf[:, :], ALU.pow), f, "rs")

            def piece(name, f):
                if name == "x0":
                    seen(pool, f, "xl", 1)
                    add_bias(f, b0b)
                elif name in ("n0", "n1", "n2"):
                    rstd(f, int(name[1]))
                elif name == "proj":
                    seen(pool, f, "tc", 2)
                    add_bias(f, bmb)
                elif name[0] == "s" and name != "sums":
                    t = int(name[1])
                    if t == 0:
                        seen(pool, f, "el", 2)
                        return
                    if t > 1:
                        seen(pool, f, "rsum", t - 1)
                    seen(pool, f, "ma", t + 1)
                    tell(pool.tensor_tensor(f["r"][:, :], (ring[0] if t == 1 else f["r"])[:, :],
                                            ring[t % 3][:, :], ALU.add), f, "rsum")

            for name, s in FIRST:
                if (name, s) == ("x0", 1):
                    for t in range(POOLED):
                        pool_mask(t)
                piece(name, turn((main, alt)[s], 0, 0, s))
            fill = filler(piece, None)
            for _ in TAIL:
                fill()

            def unit(prev, fill):
                for _ in range(BETWEEN):
                    fill()
                if prev and is_last(prev[2]):
                    pool.wait_ge(o_sems["ve"][0], prev[1] * 2 + prev[0] + 1)
                    pool.tensor_tensor(onorm[3][:, :], onorm[2][:, :], mhalf[:, :], ALU.pow
                                       ).then_inc(o_sems["rs"][0], 1)
                fill()

            with pool.Fori(0, LAST) as p:
                fill = filler(piece, p)
                for now, prev in units(p):
                    unit(prev, fill)
            for s in range(2):
                unit((s, LAST, STEPS - 1), lambda: None)

        @block.tensor
        def _(pe):
            def adj_product(dst, hi, lo, h, breaks={}):
                for t in range(T):
                    if t in breaks:
                        breaks[t]()
                    for i, (a, b) in enumerate(((hi, adj_hi), (hi, adj_lo), (lo, adj_hi))):
                        mm = pe.matmul(dst, a[:, t, :], b[:, t, cut(h)],
                                       start=(t == 0 and i == 0), stop=(t == T - 1 and i == 2))
                return mm

            def passes(dst, k, hi, lo, first, last):
                pe.matmul(dst, wh[:, k, :], hi, start=first, stop=False, skip_group_check=True)
                pe.matmul(dst, wl[:, k, :], hi, start=False, stop=False, skip_group_check=True)
                return pe.matmul(dst, wh[:, k, :], lo, start=False, stop=last, skip_group_check=True)

            def turn_half(bank, src, h):
                for j in range(HT):
                    mm = pe.transpose(ps[:, bank, tile(j)], src(h * HT + j), ident[:, :])
                return mm

            def to_natural(f, h, parts):
                for j in range(HT):
                    t = h * HT + j
                    for i, (src, k) in enumerate(parts):
                        mm = pe.matmul(ps[:, f["bank"] + h, tile(j)], src[:, tile(t)], wf[:, k, :], start=(i == 0),
                                       stop=(i == len(parts) - 1), skip_group_check=True)
                tell(mm, f, "y")

            def piece(name, f):
                bank, xs = f["bank"], xf[f["slot"]]
                if name in ("m0a", "m0b", "m1a", "m1b"):
                    n, h = int(name[1]), "ab".index(name[2])
                    if h == 0:
                        seen(pe, f, "xl", n + 1)
                    if n == 1:
                        seen(pe, f, "sum", h + 1)
                    elif f["c"]:
                        seen(pe, f, "sum", 4 + h + 1, back=1)
                    tell(adj_product(ps[:, bank + h, :], f["xh"], f["xl"], h), f, "m")
                elif name == "sums":
                    seen(pe, f, "sj", 1)
                    seen(pe, f, "mc", 3)
                    for t in range(T):
                        mm = pe.matmul(ps[:, bank, 0:2], xs[:, t, :], f["sv"][:, t, 0:2],
                                       start=(t == 0), stop=(t == T - 1))
                    tell(mm, f, "s")
                elif name == "rows":
                    seen(pe, f, "mc", 4)
                    seen(pe, f, "bc", 2)
                    for i in range(2):
                        mm = pe.matmul(ps[:, bank + 1, tile(i)], f["bc"][:, i, :], w1f[:, :], start=True, stop=True)
                    tell(mm, f, "rw")
                elif name in ("y0", "y1"):
                    n = int(name[1])
                    for h in range(2):
                        seen(pe, f, "mc", 2 * n + h + 1)
                        if n == 1:
                            seen(pe, f, "kb", 1)
                        to_natural(f, h, [(f["m"], (W0, W1R)[n])])
                elif name == "turn2":
                    seen(pe, f, "xn", 2)
                    for h in range(2):
                        tell(turn_half(bank + h, lambda t: xs[:, t, :], h), f, "t")
                elif name == "proj":
                    for h in range(2):
                        seen(pe, f, "tc", h + 1)
                        tell(pe.matmul(ps[:, bank + h, :], wf[:, WI, :], f["h"][:, cut(h)], start=True, stop=True),
                             f, "g")
                elif name == "turnh":
                    for h in range(2):
                        seen(pe, f, "el", h + 1)
                        tell(turn_half(bank + h, lambda t: f["m"][:, tile(t)], h), f, "t")
                elif name == "target":
                    for h in range(2):
                        seen(pe, f, "tc", 2 + h + 1)
                        tell(pe.matmul(ps[:, bank + h, :], we2b[:, :], f["m"][:, cut(h)], start=True, stop=True),
                             f, "at")
                elif name[0] == "e":
                    t = int(name[1])
                    if t == 0:
                        seen(pe, f, "atc", 2)
                    seen(pe, f, "ma", t + 1)
                    for h in range(2):
                        mm = pe.matmul(ps[:, bank + h, :], f["z"][:, tile(t)], ring[t % 3][:, cut(h)],
                                       start=(t == 0), stop=(t == T - 1))
                    tell(mm, f, "ag")
                elif name == "rowsum":
                    seen(pe, f, "rsum", T - 1)
                    for h in range(2):
                        seen(pe, f, "agc", h + 1)
                        tell(pe.matmul(ps[:, bank + h, :], ones[:, :], f["r"][:, cut(h)], start=True, stop=True),
                             f, "rb")
                elif name == "recv":
                    for h in range(2):
                        seen(pe, f, "self", h + 1)
                        pe.matmul(ps[:, bank + h, :], wf[:, WNA, :], f["h"][:, cut(h)], start=True, stop=False)
                        tell(pe.matmul(ps[:, bank + h, :], wf[:, WNB, :], f["v"][:, cut(h)], start=False, stop=True),
                             f, "g")
                elif name == "y2":
                    for h in range(2):
                        seen(pe, f, "el", 2 + h + 1)
                        to_natural(f, h, [(f["h"], WMA), (f["m"], WMB)])

            def turn_start(s, h, p):
                if h:
                    pe.wait_ge(n_hc[s], p * 2 + 1)
                turn_half(TB, lambda t: xf[s][:, t, :], h).then_inc(n_t[s], 1)

            def state_product(s, h, p, i, prev, breaks):
                if is_first(i):
                    pe.wait_ge(n_xl[s], p + 1)
                else:
                    pe.wait_ge(xl_done, nth_half(p, i - 1, s, 1))
                if h:
                    pe.wait_ge(ml_done, nth_half(p, i, s, 0))
                elif prev:
                    pe.wait_ge(ml_done, nth_half(*prev[1:], prev[0], 1))
                adj_product(ps[:, MB, :], xh[s], xl[s], h, breaks=breaks).then_inc(m_done, 1)

            def candidate(s, p, i):
                for h in range(2):
                    pe.wait_ge(rhl_done, nth_half(p, i, s, h))
                    passes(ps[:, VB + h, :], U5, th[s][:, cut(h)], tl[s][:, cut(h)], False, True
                           ).then_inc(v_pre, 1)

            def turn_state(s, h, p, i):
                pe.wait_ge(h_new, nth_half(p, i, s, h))
                if h:
                    pe.wait_ge(xl_done, nth_half(p, i, s, 0))
                turn_half(TB, lambda t: hT[s][:, tile(t)], h).then_inc(t_done, 1)

            def from_state(s, h, p, i, prev):
                if is_first(i):
                    pe.wait_ge(n_tl[s], p + 1)
                else:
                    pe.wait_ge(tl_done[s], p * (STEPS - 1) + i)
                if not prev:
                    seen(pe, fronts[1], "sum", 6)
                else:
                    pe.wait_ge(r_done, nth_half(*prev[1:], prev[0], h))
                passes(ps[:, GB + h, :], U3, th[s][:, cut(h)], tl[s][:, cut(h)], True, False)

            def gates(s, p, i, prev, between):
                for h in range(0 if is_first(i) else 1, 2):
                    from_state(s, h, p, i, prev)
                between()
                for h in range(2):
                    pe.wait_ge(ml_done, nth_half(p, i, s, h))
                    passes(ps[:, GB + h, :], W3, mh[:, cut(h)], ml[:, cut(h)], False, True).then_inc(z_pre, 1)
                for h in range(2):
                    if prev:
                        pe.wait_ge(v_done, nth_half(*prev[1:], prev[0], h))
                    passes(ps[:, VB + h, :], W5, mh[:, cut(h)], ml[:, cut(h)], True, False)
                for h in range(2):
                    pe.wait_ge(z_done, nth_half(p, i, s, h))
                    passes(ps[:, GB + h, :], WD, mh[:, cut(h)], ml[:, cut(h)], False, True).then_inc(r_pre, 1)

            def unit(now, prev, fill):
                s, p, i = now
                first = is_first(i)

                def in_product(h):
                    def run():
                        if first:
                            turn_start(s, h, p)
                        fill()
                    return run
                state_product(s, 0, p, i, prev, {2: in_product(0), 5: in_product(1)})
                fill()
                if prev:
                    candidate(*prev)
                fill()

                if not first:
                    from_state(s, 0, p, i, prev)

                def turn_old(h):
                    if first and h == 0:
                        pe.wait_ge(n_hc[s], p * 2 + 2)
                    if prev:
                        turn_state(prev[0], h, *prev[1:])
                state_product(s, 1, p, i, prev, {3: fill, 5: lambda: turn_old(0), 6: fill})
                fill()
                turn_old(1)
                fill()
                gates(s, p, i, prev, fill)
                fill()

            fronts = [turn((main, alt)[s], 0, 0, s) for s in range(2)]
            seen(pe, fronts[0], "xl", 1)
            for t in range(T):
                pe.wait_ge(s_al, t + 1)
                for h in range(2):
                    for i, (a, b) in enumerate(((fxh, adj_hi), (fxh, adj_lo), (fxl, adj_hi))):
                        mm = pe.matmul(ps[:, FB + h, :], a[:, t, :], b[:, t, cut(h)],
                                       start=(t == 0 and i == 0), stop=(t == T - 1 and i == 2))
                    if t == T - 1:
                        tell(mm, fronts[0], "m")
            for name, s in FIRST[4:]:
                if (name, s) == ("y0", 0):
                    pe.wait_ge(s_w0, 16)
                elif (name, s) == ("rows", 0):
                    pe.wait_ge(s_const, 6)
                    pe.wait_ge(s_wl, 1)
                piece(name, fronts[s])
            idle = lambda: None
            unit((0, 0, 0), None, filler(piece, None))
            with pe.Fori(0, LAST) as p:
                fill = filler(piece, p)
                for now, prev in units(p):
                    unit(now, prev, fill)
            last_pair(pe, unit, idle)
            end = (1, LAST, STEPS - 1)
            candidate(*end)
            for h in range(2):
                turn_state(1, h, *end[1:])

        @block.scalar
        def _(act):
            def copy(dst, src):
                return act.activation(dst, src, ACT.Copy)

            def piece(name, f):
                bank, xs = f["bank"], xf[f["slot"]]
                if name == "x0":
                    act.wait_ge(s_x[f["slot"]], f["p"] * 16 + (32 if f["c"] else 16))
                    tell(copy(f["xh"][:, :, :], xs[:, :, :]), f, "xh")
                if name in ("m0a", "m0b", "m1a", "m1b"):
                    n, h = int(name[1]), "ab".index(name[2])
                    seen(act, f, "m", 2 * n + h + 1)
                    tell(copy(f["m"][:, cut(h)], ps[:, bank + h, :]), f, "mc")
                elif name == "n0":
                    seen(act, f, "xn", 1)
                    tell(copy(f["xh"][:, :, :], xs[:, :, :]), f, "xh")
                elif name in ("turn2", "turnh"):
                    n = 0 if name == "turn2" else 2
                    for h in range(2):
                        seen(act, f, "t", n + h + 1)
                        tell(copy((f["h"] if n == 0 else f["z"])[:, cut(h)], ps[:, bank + h, :]), f, "tc")
                elif name in ("proj", "recv"):
                    n, b = (0, bi) if name == "proj" else (2, bn)
                    for h in range(2):
                        seen(act, f, "g", n + h + 1)
                        tell(act.activation(f["r"][:, cut(h)], ps[:, bank + h, :], ACT.Exp, bias=b), f, "ex")
                elif name == "target":
                    for h in range(2):
                        seen(act, f, "at", h + 1)
                        tell(copy(f["h"][:, cut(h)], ps[:, bank + h, :]), f, "atc")
                elif name[0] == "s" and name != "sums":
                    t = int(name[1])
                    if t == 0:
                        seen(act, f, "atc", 2)
                        seen(act, f, "asb", 1)
                        if f["s_e"] is alt["s_e"]:
                            seen(act, turn(main, 0, 0, 0), "ag", T)
                            seen(act, turn(main, 0, 0, 0), "rsum", T - 1)
                    if t >= 3:
                        seen(act, f, "ag", t - 2)
                        seen(act, f, "rsum", max(t - 3, 1))
                    tell(act.activation(ring[t % 3][:, :], f["h"][:, :], ACT.Sigmoid,
                                        bias=f["asrc"][:, t:t + 1]), f, "e")
                elif name == "e7":
                    seen(act, f, "ag", T)
                    for h in range(2):
                        tell(copy(f["h"][:, cut(h)], ps[:, bank + h, :]), f, "agc")

            def start_natural(s, p):
                if s == 1 and is_first(p):
                    act.wait_ge(alt["s_xn"][0], 3)
                else:
                    act.wait_ge(main["s_xn"][0], p * 6 + 3 * s if not is_first(p) else 3)
                copy(xh[s][:, :, :], xf[s][:, :, :]).then_inc(n_xh[s], 1)

            def start_turned(s, h, p):
                act.wait_ge(n_t[s], p * 2 + h + 1)
                copy(hT[s][:, cut(h)], ps[:, TB, :]).then_inc(n_hc[s], 1)

            def start_turned_hi(s, p):
                act.wait_ge(n_hc[s], p * 2 + 2)
                copy(th[s][:, :], hT[s][:, :]).then_inc(n_th[s], 1)

            def m_split(s, h, p, i):
                act.wait_ge(m_done, nth_half(p, i, s, h))
                copy(mh[:, cut(h)], ps[:, MB, :]).then_inc(mh_done, 1)

            def reset_hi(s, p, i):
                for h in range(2):
                    act.wait_ge(rh_done, nth_half(p, i, s, h))
                    copy(th[s][:, cut(h)], r[:, cut(h)]).then_inc(rhh_done, 1)

            def candidate(s, p, i):
                for h in range(2):
                    act.wait_ge(v_pre, nth_half(p, i, s, h))
                    act.activation(v[:, cut(h)], ps[:, VB + h, :], ACT.Tanh, bias=vb).then_inc(v_done, 1)

            def state_hi(s, h, p, i):
                if not is_last(i):
                    act.wait_ge(t_done, nth_half(p, i, s, h))
                    copy(nat(xh[s], h), bank4(TB)).then_inc(xh_done, 1)

            def gates(s, p, i, prev):
                if is_first(i):
                    act.wait_ge(s_out[s], p * 16 + 16)
                for h in range(2):
                    act.wait_ge(z_pre, nth_half(p, i, s, h))
                    act.activation(z[s][:, cut(h)], ps[:, GB + h, :], ACT.Sigmoid, bias=zb).then_inc(z_done, 1)
                for h in range(2):
                    act.wait_ge(r_pre, nth_half(p, i, s, h))
                    if prev:
                        act.wait_ge(rhl_done, nth_half(*prev[1:], prev[0], h))
                    act.activation(r[:, cut(h)], ps[:, GB + h, :], ACT.Sigmoid, bias=rb).then_inc(r_done, 1)

            def turned_hi(s, p, i):
                act.wait_ge(h_new, nth_half(p, i, s, 1))
                copy(th[s][:, :], hT[s][:, :]).then_inc(th_done[s], 1)

            def unit(now, prev, fill):
                s, p, i = now
                first = is_first(i)
                if first:
                    fill()
                    start_turned(s, 0, p)
                    fill()
                    start_turned(s, 1, p)
                else:
                    fill()
                    fill()
                m_split(s, 0, p, i)
                if first:
                    start_turned_hi(s, p)
                fill()
                if prev:
                    candidate(*prev)
                fill()
                fill()
                if prev:
                    state_hi(prev[0], 0, *prev[1:])
                fill()
                m_split(s, 1, p, i)
                fill()
                if prev:
                    state_hi(prev[0], 1, *prev[1:])
                fill()
                fill()
                if prev and is_last(prev[2]) and not isinstance(prev[1], int):
                    start_natural(prev[0], prev[1] + 1)
                gates(s, p, i, prev)
                if prev and not is_last(prev[2]):
                    turned_hi(*prev)
                reset_hi(s, p, i)
                fill()
                if not prev:
                    start_natural(1, p)

            begin = [(name, turn((main, alt)[s], 0, 0, s)) for name, s in FIRST]
            piece(*begin[0])
            for t in range(T):
                act.wait_ge(s_adj[t], 16)
                copy(adj_hi[:, t, :], stage[t]).then_inc(s_ah, 1)
            piece(*begin[1])
            moved = False
            for name, f in begin[2:]:
                if name == "weights":
                    act.wait_ge(s_comb, 1)
                    copy(wh[:, :, :], rflat[:, 0:5, :]).then_inc(s_wh, 1)
                elif not moved and (name == "turnh" or name == "turn2" and f["slot"] == 1):
                    act.wait_ge(s_mstore, 16 * T)
                    moved = True
                piece(name, f)
            start_natural(0, 0)
            idle = lambda: None
            unit((0, 0, 0), None, filler(piece, None))
            with act.Fori(0, LAST) as p:
                fill = filler(piece, p)
                for now, prev in units(p):
                    unit(now, prev, fill)
            last_pair(act, unit, idle)
            candidate(1, LAST, STEPS - 1)

        @block.vector
        def _(dve):
            def lo(dst, src, hi):
                return dve.tensor_tensor(dst, src, hi.bitcast(F32), ALU.subtract)

            def norm_stats(src, bufs_, wait, sig):
                st, mv, ve, _ = bufs_
                for t in range(T):
                    ins = dve.bn_stats(st[:, t, :], src[:, t, :])
                sig(ins, "st")
                m_e, m_o, q_e, q_o = (st[:, :, c] for c in (1, 4, 2, 5))
                wait("st", 1)
                sig(dve.tensor_tensor(mv[:, :, 0], m_e, m_o, ALU.add), "p1")
                sig(dve.tensor_tensor(mv[:, :, 1], m_e, m_o, ALU.subtract), "p1")
                sig(dve.tensor_tensor(ve[:, :], q_e, q_o, ALU.add), "p1")
                wait("p1", 3)
                sig(dve.scalar_tensor_tensor(out=mv[:, :, 1], in0=mv[:, :, 1], scalar=0.25, in1=mv[:, :, 1],
                                             op0=ALU.mult, op1=ALU.mult), "p2")
                sig(dve.tensor_scalar(ve[:, :], ve[:, :], 1.0 / D, EPS, ALU.mult, ALU.add), "p2")
                sig(dve.tensor_scalar(mv[:, :, 0], mv[:, :, 0], 0.5, None, ALU.mult), "mv")
                wait("p2", 2)
                sig(dve.tensor_tensor(ve[:, :], ve[:, :], mv[:, :, 1], ALU.add), "ve")

            def norm_apply(src, bufs_, wait, sig):
                _, mv, _, rs = bufs_
                wait("mv", 1)
                wait("rs", 1)
                for t in range(T):
                    ins = dve.tensor_scalar(src[:, t, :], src[:, t, :], mv[:, t, 0:1], rs[:, t:t + 1],
                                            ALU.subtract, ALU.mult)
                sig(ins, "xn")

            def f_wait(f, n):
                def wait(name, c):
                    per = f["s_" + name][1] // 3
                    seen(dve, f, name, n * per + c)
                return wait

            def row_dots(junk, src, row, col):
                for t in range(T):
                    ins = dve.tensor_tensor_reduce(out=junk[:, tile(t)], in0=src[:, t, :], in1=row, scale=1.0,
                                                   scalar=0.0, op0=ALU.mult, op1=ALU.add, accum_out=col(t))
                return ins

            def elu(f, n, b, dst):
                for h in range(2):
                    seen(dve, f, "ex", n + h + 1)
                    tell(dve.tensor_scalar(f["r"][:, cut(h)], f["r"][:, cut(h)], 1.0, 1.0, ALU.min, ALU.subtract),
                         f, "em")
                    seen(dve, f, "em", n + h + 1)
                    tell(dve.scalar_tensor_tensor(out=dst[:, cut(h)], in0=ps[:, f["bank"] + h, :], scalar=b,
                                                  in1=f["r"][:, cut(h)], op0=ALU.add, op1=ALU.max), f, "el")

            def piece(name, f):
                bank, xs = f["bank"], xf[f["slot"]]
                if name == "x0":
                    seen(dve, f, "xh", 1)
                    tell(lo(f["xl"][:, :, :], xs[:, :, :], f["xh"][:, :, :]), f, "xl")
                elif name in ("y0", "y1", "y2"):
                    n = int(name[1])
                    if n == 0:
                        seen(dve, f, "xb", 1)
                    elif n == 1:
                        seen(dve, f, "kbx", 1)
                    else:
                        seen(dve, f, "xb", 2)
                    for h in range(2):
                        seen(dve, f, "y", 2 * n + h + 1)
                        tell(dve.tensor_tensor(nat(xs, h), bank4(bank + h), nat(xs, h), ALU.add), f, "sum")
                elif name in ("v0", "v1", "v2"):
                    n = int(name[1])
                    seen(dve, f, "sum", 2 * n + 2)
                    norm_stats(xs, f["norm"], f_wait(f, n), lambda ins, k: tell(ins, f, k))
                elif name in ("n0", "n1", "n2"):
                    n = int(name[1])
                    norm_apply(xs, f["norm"], f_wait(f, n), lambda ins, k: tell(ins, f, k))
                    if n == 0:
                        seen(dve, f, "xh", 2)
                        tell(lo(f["xl"][:, :, :], xs[:, :, :], f["xh"][:, :, :]), f, "xl")
                elif name == "m1a":
                    row_dots(f["v"], xs, wjb, lambda t: f["sv"][:, t, 1:2])
                    tell(row_dots(f["r"], xs, wib, lambda t: f["sv"][:, t, 2:3]), f, "sj")
                elif name == "sums":
                    seen(dve, f, "s", 1)
                    sc = f["sc"]
                    tell(dve.tensor_copy(sc[:, :], ps[:, bank, 0:2]), f, "sc")
                    seen(dve, f, "sc", 1)
                    tell(dve.scalar_tensor_tensor(out=sc[:, 1:2], in0=sc[:, 0:1], scalar=gb, in1=sc[:, 1:2],
                                                  op0=ALU.mult, op1=ALU.add), f, "k")
                    seen(dve, f, "k", 1)
                    for i in range(2):
                        tell(dve.tensor_scalar(f["bc"][:, i, :], ones[:, :], sc[:, i:i + 1], None, ALU.mult),
                             f, "bc")
                elif name == "rows":
                    seen(dve, f, "rw", 1)
                    for t in range(T):
                        ins = dve.scalar_tensor_tensor(out=xs[:, t, :], in0=ps[:, bank + 1, 0:P],
                                                       scalar=f["sv"][:, t, 2:3], in1=xs[:, t, :],
                                                       op0=ALU.mult, op1=ALU.add)
                    tell(ins, f, "rx")
                    tell(dve.tensor_tensor(f["kb"][:, :], ps[:, bank + 1, P:2 * P], b1b, ALU.add), f, "kb")
                    seen(dve, f, "rx", 1)
                    seen(dve, f, "kb", 1)
                    tell(dve.tensor_tensor(xs[:, :, :], xs[:, :, :],
                                           f["kb"][:, :].unsqueeze(1).to_broadcast([P, T, D]), ALU.add), f, "kbx")
                elif name == "proj":
                    elu(f, 0, bi, f["m"])
                elif name == "turnh":
                    seen(dve, f, "tc", 4)
                    tell(row_dots(f["v"], f["z"][:, :].rearrange("p (t d) -> p t d", d=D), we1b,
                                  lambda t: f["asrc"][:, t:t + 1]), f, "as")
                    seen(dve, f, "as", 1)
                    tell(dve.tensor_scalar(f["asrc"][:, :], f["asrc"][:, :], be, None, ALU.add), f, "asb")
                elif name == "recv":
                    elu(f, 2, bn, f["h"])
                elif name == "rowsum":
                    for h in range(2):
                        seen(dve, f, "rb", h + 1)
                        tell(dve.tensor_tensor(f["v"][:, cut(h)], ps[:, bank + h, :], f["m"][:, cut(h)], ALU.mult),
                             f, "self")
                elif name[0] == "s":
                    t = int(name[1])
                    if f["s_e"] is alt["s_e"]:
                        dve.wait_ge(s_mk[t % 2], 16 * (T // 2 + t // 2 + 1))
                    else:
                        before = (f["c"] + 1 if f["c"] else 0) * T // 2
                        dve.wait_ge(s_mk[t % 2], f["p"] * (16 * T) + 16 * (before + t // 2 + 1))
                    seen(dve, f, "e", t + 1)
                    tell(dve.tensor_tensor(ring[t % 3][:, :], ring[t % 3][:, :], mk[t % 2][:, :], ALU.mult),
                         f, "ma")

            def start_natural(s, p):
                dve.wait_ge(n_xh[s], p + 1)
                lo(xl[s][:, :, :], xf[s][:, :, :], xh[s][:, :, :]).then_inc(n_xl[s], 1)
                if not is_first(p):
                    dve.wait_ge(xl_done, nth_half(p, -1, s, 1))
                dve.tensor_copy(x[s][:, :, :], xf[s][:, :, :]).then_inc(n_x[s], 1)

            def start_turned(s, p):
                dve.wait_ge(n_th[s], p + 1)
                lo(tl[s][:, :], hT[s][:, :], th[s][:, :]).then_inc(n_tl[s], 1)

            def m_split(s, h, p, i):
                dve.wait_ge(mh_done, nth_half(p, i, s, h))
                lo(ml[:, cut(h)], ps[:, MB, :], mh[:, cut(h)]).then_inc(ml_done, 1)

            def reset(s, p, i):
                for h in range(2):
                    dve.wait_ge(r_done, nth_half(p, i, s, h))
                    dve.tensor_tensor(r[:, cut(h)], r[:, cut(h)], hT[s][:, cut(h)], ALU.mult).then_inc(rh_done, 1)

            def reset_lo(s, p, i):
                for h in range(2):
                    dve.wait_ge(rhh_done, nth_half(p, i, s, h))
                    lo(tl[s][:, cut(h)], r[:, cut(h)], th[s][:, cut(h)]).then_inc(rhl_done, 1)

            def update(s, p, i):
                for h in range(2):
                    dve.wait_ge(v_done, nth_half(p, i, s, h))
                    dve.tensor_tensor(v[:, cut(h)], v[:, cut(h)], hT[s][:, cut(h)], ALU.subtract).then_inc(d_sub, 1)
                    dve.wait_ge(d_sub, nth_half(p, i, s, h))
                    dve.tensor_tensor(v[:, cut(h)], v[:, cut(h)], z[s][:, cut(h)], ALU.mult).then_inc(d_mul, 1)
                    dve.wait_ge(d_mul, nth_half(p, i, s, h))
                    dve.tensor_tensor(hT[s][:, cut(h)], hT[s][:, cut(h)], v[:, cut(h)], ALU.add).then_inc(h_new, 1)

            def state_lo(s, h, p, i):
                if is_last(i):
                    dve.wait_ge(t_done, nth_half(p, i, s, h))
                    dve.tensor_tensor(nat(zflat[s], h), bank4(TB), nat(x[s], h), ALU.add).then_inc(xl_done, 1)
                else:
                    dve.wait_ge(xh_done, p * (4 * (STEPS - 1)) + i * 4 + (2 * s + h + 1))
                    lo(nat(xl[s], h), bank4(TB), nat(xh[s], h)).then_inc(xl_done, 1)

            def turned_lo(s, p, i):
                dve.wait_ge(th_done[s], p * (STEPS - 1) + i + 1)
                lo(tl[s][:, :], hT[s][:, :], th[s][:, :]).then_inc(tl_done[s], 1)

            def unit(now, prev, fill):
                s, p, i = now
                first = is_first(i)
                fill()
                fill()
                m_split(s, 0, p, i)
                if first:
                    start_turned(s, p)
                fill()
                if prev:
                    update(*prev)
                fill()
                fill()
                if prev:
                    state_lo(prev[0], 0, *prev[1:])
                fill()
                m_split(s, 1, p, i)
                fill()
                if prev:
                    state_lo(prev[0], 1, *prev[1:])
                fill()
                fill()
                if prev and is_last(prev[2]) and not isinstance(prev[1], int):
                    start_natural(prev[0], prev[1] + 1)
                if prev and is_last(prev[2]):
                    stats, apply = output(*prev[:2])
                    stats()
                reset(s, p, i)
                if prev and not is_last(prev[2]):
                    turned_lo(*prev)
                reset_lo(s, p, i)
                if prev and is_last(prev[2]):
                    apply()
                fill()
                if not prev:
                    start_natural(1, p)

            def output(s, p):
                o_wait = lambda name, c: dve.wait_ge(o_sems[name][0], p * (2 * o_sems[name][1])
                                                     + (s * o_sems[name][1] + c))
                o_tell = lambda ins, name: ins.then_inc(o_sems[name][0], 1)

                def stats():
                    dve.wait_ge(xl_done, nth_half(p, STEPS - 1, s, 1))
                    norm_stats(zflat[s], onorm, o_wait, o_tell)
                return stats, lambda: norm_apply(zflat[s], onorm, o_wait, o_tell)

            begin = [(name, turn((main, alt)[s], 0, 0, s)) for name, s in FIRST]
            piece(*begin[0])
            for t in range(T):
                dve.wait_ge(s_ah, t + 1)
                lo(adj_lo[:, t, :], stage[t], adj_hi[:, t, :]).then_inc(s_al, 1)
            piece(*begin[1])

            def weights():
                dve.wait_ge(s_w, 16 * W_LOADS)
                dve.wait_ge(s_wv, 16 * V_LOADS)
                for s in range(2):
                    dve.wait_ge(s_out[s], 16)
                for k, half in ((W3, 0), (5, 2), (W5, 4)):
                    dve.tensor_tensor(rflat[:, k, :], zflat[1][:, half, :], zflat[1][:, half + 1, :], ALU.add
                                      ).then_inc(s_comb0, 1)
                dve.tensor_tensor(zb, w3b, u3b, ALU.add).then_inc(s_comb0, 1)
                dve.tensor_tensor(rb, w4b, u3b, ALU.add).then_inc(s_comb0, 1)
                dve.tensor_tensor(vb, w5b, u5b, ALU.add).then_inc(s_comb0, 1)
                dve.wait_ge(s_const, 6)
                dve.tensor_scalar(we2b[:, :], ones[:, :], we2, None, ALU.mult).then_inc(s_comb0, 1)
                dve.tensor_scalar(wf[:, W1R, :], w1f[:, :], wr, None, ALU.mult).then_inc(s_comb0, 1)
                dve.wait_ge(s_comb0, 8)
                dve.tensor_tensor(rflat[:, WD, :], rflat[:, 5, :], rflat[:, W3, :], ALU.subtract).then_inc(s_comb, 1)
                dve.wait_ge(s_wh, 1)
                lo(wl[:, :, :], rflat[:, 0:5, :], wh[:, :, :]).then_inc(s_wl, 1)

            for name, f in begin[2:]:
                if name == "weights":
                    weights()
                elif name[:4] == "mask":
                    t = int(name[4])
                    n = t - POOLED
                    if n:
                        dve.wait_ge(s_mask, n)
                    dve.tensor_scalar(noedge[:, :], stage[t], 0.0, ALPHA, ALU.is_equal, ALU.mult
                                      ).then_inc(s_noedge, 1)
                    dve.wait_ge(s_noedge, n + 1)
                    dve.tensor_tensor(stage[t], stage[t], noedge[:, :], ALU.add).then_inc(s_mask, 1)
                    if t == T - 1:
                        dve.wait_ge(s_mask, T - POOLED)
                        dve.wait_ge(s_pmask, POOLED)
                piece(name, f)
            dve.wait_ge(s_mstore, 16 * T)
            start_natural(0, 0)
            idle = lambda: None
            unit((0, 0, 0), None, filler(piece, None))
            with dve.Fori(0, LAST) as p:
                fill = filler(piece, p)
                for now, prev in units(p):
                    unit(now, prev, fill)
            last_pair(dve, unit, idle)
            end = (1, LAST, STEPS - 1)
            update(*end)
            for h in range(2):
                state_lo(1, h, *end[1:])
            for part in output(*end[:2]):
                part()


def kernel(**inputs):
    import numpy as _np
    import concourse.bacc as _bacc
    from concourse import mybir as _mybir
    from concourse.bass_utils import run_bass_kernel_spmd as _run

    a = {k: _np.asarray(v) for k, v in inputs.items()}
    D = a["x"].shape[2]
    lay = {
        "x": a["x"], "adjT": a["adj"].T,
        "W0": a["L0_gnn_weight"], "W1": a["L1_gnn_weight"],
        "W2": _np.concatenate([a["L2_gnn_Wi"], a["L2_gnn_Wn"][:D], a["L2_gnn_Wn"][D:], a["L2_gnn_Wm"][:D],
                               a["L2_gnn_Wm"][D:]], axis=1),
        "halves": _np.concatenate([a[f"L3_gnn_w{k}_w"][:, h * D:(h + 1) * D].T for k in (3, 4, 5)
                                   for h in range(2)], axis=1),
        "u3": a["L3_gnn_u3_w"].T, "u5": a["L3_gnn_u5_w"].T,
        "columns": _np.concatenate([v.reshape(D, 1) for v in (
            a["L2_gnn_We"][D:], a["L2_gnn_bi"], a["L2_gnn_bn"], a["L3_gnn_w3_b"], a["L3_gnn_w4_b"],
            a["L3_gnn_u3_b"], a["L3_gnn_w5_b"], a["L3_gnn_u5_b"])], axis=1),
        "scalars": _np.concatenate([v.reshape(1, 1) for v in (
            a["L1_gnn_g_w"][2 * D:], a["L1_gnn_g_b"], a["L2_gnn_be"])], axis=1),
        "rows": _np.concatenate([v.reshape(1, D) for v in (
            a["L0_gnn_bias"], a["L1_gnn_bias"], a["L2_gnn_bm"], a["L1_gnn_g_w"][:D], a["L1_gnn_g_w"][D:2 * D],
            a["L2_gnn_We"][:D])], axis=1),
    }
    nc = _bacc.Bacc("TRN2", target_bir_lowering=False, num_devices=1)
    arrays, aps = {}, {}
    for name, v in lay.items():
        v = _np.ascontiguousarray(v)
        arrays[f"in_{name}"] = v
        aps[name] = nc.dram_tensor(f"in_{name}", v.shape, _mybir.dt.from_np(v.dtype), kind="ExternalInput").ap()
    out = nc.dram_tensor("out", a["x"].shape, _mybir.dt.from_np(a["x"].dtype), kind="ExternalOutput").ap()
    mask = nc.dram_tensor("mask_scratch", a["adj"].shape, _mybir.dt.float32, kind="Internal").ap()
    program(nc, aps["x"], aps["adjT"], aps, mask, out)
    res = _run(nc, [arrays], core_ids=[0])
    return res.results[0]["out"]
```
